# Optimizing a Trainium2 kernel written in Bass

```python
import numpy as np
import jax
import jax.numpy as jnp

def _softmax(x, axis=-1):
    return jax.nn.softmax(x, axis=axis)

def _gelu(x):
    return jax.nn.gelu(x, approximate=True)

def _silu(x):
    return jax.nn.silu(x)

def _sigmoid(x):
    return jax.nn.sigmoid(x)

def _layernorm(x, axis=-1, eps=1e-05):
    m = jnp.mean(x, axis=axis, keepdims=True)
    v = jnp.var(x, axis=axis, keepdims=True)
    return (x - m) / jnp.sqrt(v + eps)

def _scatter_add(tgt, idx, src, axis=0):
    return tgt.at[idx].add(src)

def _segment_sum(src, seg, n):
    return jax.ops.segment_sum(src, seg, n)
kernel_name = 'mk_macaron_d1_jaxref_r8_d90e26'

def setup_inputs(seed: int=0):
    np.random.seed(seed)
    _w = jnp.asarray

    def _L0_attn_setup():
        import jax, jax.numpy as jnp
        import numpy as np
        D_MODEL = 128
        N_HEADS = 16
        D_HEAD = 64
        VAR_EPS = 1e-05
        INIT_RANGE = 0.02
        B, S = (2, 256)

        def _layernorm(x, w, b):
            mean = jnp.mean(x, axis=-1, keepdims=True)
            var = jnp.var(x, axis=-1, keepdims=True)
            norm = (x - mean) / jnp.sqrt(var + VAR_EPS)
            return norm * w + b
        key = jax.random.key(seed)
        ks = jax.random.split(key, 6)
        resid_stream = jax.random.normal(ks[0], (B, S, D_MODEL), dtype=jnp.float32)
        attn_mask = jnp.ones((B, S), dtype=jnp.int32)
        W_q = jax.random.normal(ks[1], (N_HEADS, D_MODEL, D_HEAD), dtype=jnp.float32) * INIT_RANGE
        W_k = jax.random.normal(ks[2], (N_HEADS, D_MODEL, D_HEAD), dtype=jnp.float32) * INIT_RANGE
        W_v = jax.random.normal(ks[3], (N_HEADS, D_MODEL, D_HEAD), dtype=jnp.float32) * INIT_RANGE
        W_o = jax.random.normal(ks[4], (N_HEADS, D_HEAD, D_MODEL), dtype=jnp.float32) * INIT_RANGE
        b_q = jnp.zeros((N_HEADS, D_HEAD), dtype=jnp.float32)
        b_k = jnp.zeros((N_HEADS, D_HEAD), dtype=jnp.float32)
        b_v = jnp.zeros((N_HEADS, D_HEAD), dtype=jnp.float32)
        b_o = jnp.zeros((D_MODEL,), dtype=jnp.float32)
        ln_w = jnp.ones((D_MODEL,), dtype=jnp.float32)
        ln_b = jnp.zeros((D_MODEL,), dtype=jnp.float32)
        return dict(resid_stream=resid_stream, attn_mask=attn_mask, W_q=W_q, W_k=W_k, W_v=W_v, W_o=W_o, b_q=b_q, b_k=b_k, b_v=b_v, b_o=b_o, ln_w=ln_w, ln_b=ln_b)
    _L0_attn_in = _L0_attn_setup()

    def _L0_ffn_setup():
        import jax, jax.numpy as jnp
        import numpy as np
        MICRO_BATCHES = 2
        TOP_K = 2
        LN_EPS = 1e-05
        B, S, D = (4, 512, 128)
        E = 8
        DFF = 4 * D

        def _layernorm(x, g, b):
            mu = jnp.mean(x, axis=-1, keepdims=True)
            var = jnp.mean(jnp.square(x - mu), axis=-1, keepdims=True)
            return (x - mu) * jax.lax.rsqrt(var + LN_EPS) * g + b
        key = jax.random.key(seed)
        ks = jax.random.split(key, 12)
        sd = 1.0 / np.sqrt(D)
        sf = 1.0 / np.sqrt(DFF)
        return {'x': jax.random.normal(ks[0], (B, S, D), dtype=jnp.float32), 'ln_g': jnp.ones((D,), jnp.float32), 'ln_b': jnp.zeros((D,), jnp.float32), 'attn_w': jax.random.normal(ks[1], (D, D), jnp.float32) * sd, 'attn_b': jnp.zeros((D,), jnp.float32), 'gate_w': jax.random.normal(ks[2], (D, E), jnp.float32) * sd, 'w1': jax.random.normal(ks[3], (E, D, DFF), jnp.float32) * sd, 'b1': jnp.zeros((E, DFF), jnp.float32), 'w2': jax.random.normal(ks[4], (E, DFF, D), jnp.float32) * sf, 'b2': jnp.zeros((E, D), jnp.float32), 'next_w': jax.random.normal(ks[5], (D, D), jnp.float32) * sd, 'next_b': jnp.zeros((D,), jnp.float32)}
    _L0_ffn_in = _L0_ffn_setup()
    _d = {'L0_attn_resid_stream': _L0_attn_in['resid_stream'], 'L0_attn_attn_mask': _L0_attn_in['attn_mask'], 'L0_attn_W_q': _L0_attn_in['W_q'], 'L0_attn_W_k': _L0_attn_in['W_k'], 'L0_attn_W_v': _L0_attn_in['W_v'], 'L0_attn_W_o': _L0_attn_in['W_o'], 'L0_attn_b_q': _L0_attn_in['b_q'], 'L0_attn_b_k': _L0_attn_in['b_k'], 'L0_attn_b_v': _L0_attn_in['b_v'], 'L0_attn_b_o': _L0_attn_in['b_o'], 'L0_attn_ln_w': _L0_attn_in['ln_w'], 'L0_attn_ln_b': _L0_attn_in['ln_b'], 'L0_ffn_ln_g': _L0_ffn_in['ln_g'], 'L0_ffn_ln_b': _L0_ffn_in['ln_b'], 'L0_ffn_attn_w': _L0_ffn_in['attn_w'], 'L0_ffn_attn_b': _L0_ffn_in['attn_b'], 'L0_ffn_gate_w': _L0_ffn_in['gate_w'], 'L0_ffn_w1': _L0_ffn_in['w1'], 'L0_ffn_b1': _L0_ffn_in['b1'], 'L0_ffn_w2': _L0_ffn_in['w2'], 'L0_ffn_b2': _L0_ffn_in['b2'], 'L0_ffn_next_w': _L0_ffn_in['next_w'], 'L0_ffn_next_b': _L0_ffn_in['next_b']}
    _x0 = _d['L0_attn_resid_stream']
    _d['L0_attn_resid_stream'] = jax.random.normal(jax.random.fold_in(jax.random.key(seed), 1), (4, 512, 128), dtype=_x0.dtype)
    del _x0
    return _d

def reference(L0_attn_resid_stream, L0_attn_attn_mask, L0_attn_W_q, L0_attn_W_k, L0_attn_W_v, L0_attn_W_o, L0_attn_b_q, L0_attn_b_k, L0_attn_b_v, L0_attn_b_o, L0_attn_ln_w, L0_attn_ln_b, L0_ffn_ln_g, L0_ffn_ln_b, L0_ffn_attn_w, L0_ffn_attn_b, L0_ffn_gate_w, L0_ffn_w1, L0_ffn_b1, L0_ffn_w2, L0_ffn_b2, L0_ffn_next_w, L0_ffn_next_b):

    def _L0_attn_ref(resid_stream, attn_mask, W_q, W_k, W_v, W_o, b_q, b_k, b_v, b_o, ln_w, ln_b):
        import jax, jax.numpy as jnp
        import numpy as np
        D_MODEL = 128
        N_HEADS = 16
        D_HEAD = 64
        VAR_EPS = 1e-05
        INIT_RANGE = 0.02
        B, S = (2, 256)

        def _layernorm(x, w, b):
            mean = jnp.mean(x, axis=-1, keepdims=True)
            var = jnp.var(x, axis=-1, keepdims=True)
            norm = (x - mean) / jnp.sqrt(var + VAR_EPS)
            return norm * w + b
        x = _layernorm(resid_stream, ln_w, ln_b)
        q = jnp.einsum('bsd,hde->bshe', x, W_q) + b_q
        k = jnp.einsum('bsd,hde->bshe', x, W_k) + b_k
        v = jnp.einsum('bsd,hde->bshe', x, W_v) + b_v
        scale = D_HEAD ** (-0.5)
        scores = jnp.einsum('bqhe,bkhe->bhqk', q, k) * scale
        sq, sk = (scores.shape[-2], scores.shape[-1])
        causal = jnp.tril(jnp.ones((sq, sk), dtype=bool))
        scores = jnp.where(causal, scores, -jnp.inf)
        pattern = jax.nn.softmax(scores, axis=-1)
        z = jnp.einsum('bhqk,bkhe->bqhe', pattern, v)
        attn_out = jnp.einsum('bqhe,hed->bqd', z, W_o) + b_o
        return attn_out

    def _L0_ffn_ref(x, ln_g, ln_b, attn_w, attn_b, gate_w, w1, b1, w2, b2, next_w, next_b):
        import jax, jax.numpy as jnp
        import numpy as np
        MICRO_BATCHES = 2
        TOP_K = 2
        LN_EPS = 1e-05
        B, S, D = (4, 512, 128)
        E = 8
        DFF = 4 * D

        def _layernorm(x, g, b):
            mu = jnp.mean(x, axis=-1, keepdims=True)
            var = jnp.mean(jnp.square(x - mu), axis=-1, keepdims=True)
            return (x - mu) * jax.lax.rsqrt(var + LN_EPS) * g + b
        Bx, Sx, Dx = x.shape
        N = Bx * Sx
        x_flat = x.reshape(N, Dx)
        x_attn = _layernorm(x_flat, ln_g, ln_b) @ attn_w + attn_b + x_flat
        logits = x_attn @ gate_w
        _ = jax.lax.top_k(logits, TOP_K)
        tpe = N // (MICRO_BATCHES * E)
        g = x_attn.reshape(MICRO_BATCHES, E, tpe, Dx)
        h = jax.nn.gelu(jnp.einsum('metd,edf->metf', g, w1) + b1[None, :, None, :], approximate=False)
        y = jnp.einsum('metf,efd->metd', h, w2) + b2[None, :, None, :]
        out = jax.nn.gelu(y @ next_w + next_b, approximate=False)
        return out.reshape(Bx, Sx, Dx)
    x = L0_attn_resid_stream
    x = x + 0.5 * _L0_ffn_ref(_layernorm(x, axis=-1), L0_ffn_ln_g, L0_ffn_ln_b, L0_ffn_attn_w, L0_ffn_attn_b, L0_ffn_gate_w, L0_ffn_w1, L0_ffn_b1, L0_ffn_w2, L0_ffn_b2, L0_ffn_next_w, L0_ffn_next_b)
    x = x + _L0_attn_ref(_layernorm(x, axis=-1), L0_attn_attn_mask, L0_attn_W_q, L0_attn_W_k, L0_attn_W_v, L0_attn_W_o, L0_attn_b_q, L0_attn_b_k, L0_attn_b_v, L0_attn_b_o, L0_attn_ln_w, L0_attn_ln_b)
    x = x + 0.5 * _L0_ffn_ref(_layernorm(x, axis=-1), L0_ffn_ln_g, L0_ffn_ln_b, L0_ffn_attn_w, L0_ffn_attn_b, L0_ffn_gate_w, L0_ffn_w1, L0_ffn_b1, L0_ffn_w2, L0_ffn_b2, L0_ffn_next_w, L0_ffn_next_b)
    return x

_drawn_inputs = setup_inputs


def setup_inputs(seed=0):
    import zlib

    import numpy as np

    out = dict(_drawn_inputs(seed))
    spreads = {'L0_attn_b_q': (0.0, 0.8),
     'L0_attn_b_k': (0.0, 0.8),
     'L0_attn_b_v': (0.0, 0.1),
     'L0_attn_b_o': (0.0, 0.1),
     'L0_attn_ln_w': (1.0, 0.6),
     'L0_attn_ln_b': (0.0, 0.625),
     'L0_ffn_ln_g': (1.0, 0.2),
     'L0_ffn_ln_b': (0.0, 0.1),
     'L0_ffn_attn_b': (0.0, 0.1),
     'L0_ffn_b1': (0.0, 0.1),
     'L0_ffn_b2': (0.0, 0.1),
     'L0_ffn_next_b': (0.0, 0.1)}
    factors = {'L0_attn_W_q': 8.0, 'L0_attn_W_k': 8.0}
    for name, (base, spread) in spreads.items():
        noise = np.random.default_rng([zlib.crc32(name.encode()), seed]).standard_normal(out[name].shape)
        drawn = base * np.exp(spread * noise) if base else spread * noise
        out[name] = jnp.asarray(drawn.astype(out[name].dtype))
    for name, factor in factors.items():
        out[name] = (out[name] * factor).astype(out[name].dtype)
    return out
```

```python
from contextlib import ExitStack

import concourse.bass as bass
from concourse import mybir

ALU = mybir.AluOpType
ACT = mybir.ActivationFunctionType
F32 = mybir.dt.float32
F32R = mybir.dt.float32r

P = 128
EPS = 1e-5
NEG = -1e30
BIG = 3e38


def macaron_kernel(nc, resid, W_q, W_k, W_v, W_o, b_q, b_k, b_v, b_o, aln_w, aln_b,
                   ln_g, ln_b, attn_w, attn_b, w1, b1, w2, b2, next_w, next_b, out):
    B, S, D = resid.shape
    H, _, DH = W_q.shape
    E, _, DFF = w1.shape
    NT = B * S // P
    TB = S // P
    FC = DFF // P
    NP = H // 2
    MB = NT // E
    G = B * NP
    SCALE = DH ** -0.5
    CPP = 2 * TB
    assert D == P and 2 * DH == P and S == 512 and MB == 2 and TB == 4 and NP == 8

    PT_CHUNKS = [[(0, 0)], [(1, 0), (3, 384)], [(2, 0)]]
    PT_WIDTH = [512, 512, 256]
    PT_AT = [0, 512, 1024]
    PT_OF_KEY = {0: 0, 1: 512, 3: 896, 2: 1024}
    Q_AT = [0, 128, 384, 768]
    HW = 1280
    NW = 4

    C_LNG, C_LNB, C_ATTNB, C_NEXTB, C_ALNW, C_ALNB = range(6)
    C_B2 = 6
    C_B1 = C_B2 + E
    C_BQ = C_B1 + E * FC
    C_BK = C_BQ + NP
    NCONST = C_BK + NP

    PEELED = 5
    PAIRS_OF_SEQUENCES = ((0, 2), (1, 3))

    def misc(b, p, what):
        if isinstance(b, int) and b == 0 and p < 2:
            return 4 + 4 * p + ("k", "q", "v", "x").index(what)
        if p < 2:
            return b * 26 + (4 + 3 * p + ("k", "q", "v", "out").index(what))
        if p == 2:
            return b * 26 + (11 + ("out", "k", "q", "v").index(what))
        return b * 26 + (15 + 3 * (p - 3) + ("k", "q", "v").index(what))

    LAST_OUT = misc(B - 1, 6, "v")

    NORMS = [(b, which) for pair in PAIRS_OF_SEQUENCES for which in (0, 1) for b in pair]
    NORMS += [(0, 0), (2, 0), (0, 1), (2, 1), (1, 0), (1, 1), (3, 0), (3, 1)]
    LOOP_NORMS = len(NORMS)

    def norms_up_to(phase, b, which):
        if phase < 2:
            return NORMS.index((b, which), 8 * phase) + 1
        return LOOP_NORMS + 2 * b + which + 1

    with ExitStack() as ctx:
        def sb(name, shape, dt=F32):
            return ctx.enter_context(nc.sbuf_tensor(name, shape, dt))

        def sem(name):
            return ctx.enter_context(nc.semaphore(name))

        banks = [ctx.enter_context(nc.psum_tensor(f"bank{i}", [P, 512], F32)) for i in range(8)]

        ident = sb("ident", [P, P])
        mask = sb("mask", [P, S])
        const_rows = sb("const_rows", [NCONST, P])
        consts = sb("consts", [P, NCONST])
        half_pow = sb("half_pow", [P, TB])
        bv_row = sb("bv_row", [P, H * DH])
        bo_row = sb("bo_row", [P, D])
        wproj_hi = sb("wproj_hi", [P, 3, H * DH], F32R)
        wproj_lo = sb("wproj_lo", [P, 3, H * DH], F32R)
        wo = sb("wo", [P, NP, D])
        wattn = sb("wattn", [P, D])
        wnext = sb("wnext", [P, D])
        w1_sb = sb("w1_sb", [P, NW, DFF])
        w2_sb = sb("w2_sb", [P, NW, FC, D])

        x_res = sb("x_res", [P, NT, D])
        x_norm = sb("x_norm", [P, NT, D])
        x_norm2 = sb("x_norm2", [P, NT, D])
        stats = sb("stats", [P, 2, TB, 6])
        st_sum, st_diff, st_m2, st_mean, st_diff2, st_var4, st_var, st_rstd = (
            sb(f"st_{name}", [P, 2, TB]) for name in ("sum", "diff", "m2", "mean", "diff2", "var4", "var", "rstd"))

        xT = sb("xT", [P, B, S])
        x0T = sb("x0T", [P, B, S])
        xT_hi = sb("xT_hi", [P, B, S], F32R)
        xT_lo = sb("xT_lo", [P, B, S], F32R)
        xcur_hi = sb("xcur_hi", [P, S], F32R)
        xcur_lo = sb("xcur_lo", [P, S], F32R)
        oT = sb("oT", [P, 2, S])

        q_hi = sb("q_hi", [P, 2, S], F32R)
        q_lo = sb("q_lo", [P, 2, S], F32R)
        k_hi = sb("k_hi", [P, 2, S], F32R)
        k_lo = sb("k_lo", [P, 2, S], F32R)
        v_sb = sb("v_sb", [P, TB, H * DH])
        prob = sb("prob", [P, 2, 2, HW])
        probT = sb("probT", [P, 2, 2, HW])
        wproj = probT[:].rearrange("p a b c -> p (a b c)")[:, 0:3 * H * DH].rearrange("p (i c) -> p i c", i=3)
        hT = prob[:].rearrange("p a b c -> p (a b c)")[:, 0:2 * FC * MB * P].rearrange("p (a c t) -> p a c t", a=2, c=FC)
        yT = x_norm[:].rearrange("p (b t) d -> p b (t d)", b=B)
        neg_max = sb("neg_max", [P, 2, CPP])
        row_sum = sb("row_sum", [P, 2, CPP])
        row_rec = sb("row_rec", [P, 2, CPP])
        zT = sb("zT", [P, NP, S])

        x_in = sem("x_in")
        rows_in = sem("rows_in")
        bv_in = sem("bv_in")
        bo_in = sem("bo_in")
        bo_added = sem("bo_added")
        wproj_in = sem("wproj_in")
        wo_in = sem("wo_in")
        wdense_in = sem("wdense_in")
        expert_in = [sem(f"expert_in{i}") for i in range(NW)]
        pool_init = sem("pool_init")
        ident_ready = sem("ident_ready")
        mask_ready = sem("mask_ready")
        wsplit_hi = sem("wsplit_hi")
        wsplit_ready = sem("wsplit_ready")
        consts_T = sem("consts_T")
        consts_ready = sem("consts_ready")
        stats_done = sem("stats_done")
        norm_math = sem("norm_math")
        var_ready = sem("var_ready")
        rstd_ready = sem("rstd_ready")
        normed = sem("normed")
        nT_full = sem("nT_full")
        x0T_full = sem("x0T_full")
        nT_ready = sem("nT_ready")
        x0T_ready = sem("x0T_ready")
        attn_full = sem("attn_full")
        xattn_ready = sem("xattn_ready")
        h_full = sem("h_full")
        h_ready = sem("h_ready")
        y_full = sem("y_full")
        y_ready = sem("y_ready")
        next_full = sem("next_full")
        o_ready = sem("o_ready")
        oback_full = sem("oback_full")
        resid_done = sem("resid_done")
        out_done = sem("out_done")
        xin_full = sem("xin_full")
        xin_ready = sem("xin_ready")
        xhi_ready = sem("xhi_ready")
        xlo_ready = sem("xlo_ready")
        xcur_in = sem("xcur_in")
        misc_full = sem("misc_full")
        misc_free = sem("misc_free")
        qk_hi_ready = sem("qk_hi_ready")
        s_full = sem("s_full")
        s_masked = sem("s_masked")
        exp_done = sem("exp_done")
        rec_ready = sem("rec_ready")
        prob_ready = sem("prob_ready")
        pt_full = [sem("pt_full0"), sem("pt_full1")]
        pt_evac = [sem("pt_evac0"), sem("pt_evac1")]
        pv_done = sem("pv_done")
        z_ready = sem("z_ready")

        MISC = banks[0]
        SCORE = banks[1:5]
        PT = banks[5:7]
        ZT = banks[7]
        X0_BANK = [banks[1], banks[3]]
        N_BANK = [banks[2], banks[4]]
        H_BANK = [banks[5:7], (banks[0], banks[7])]
        Y_BANK = [banks[1], banks[2]]
        O_BANK = [banks[0], banks[7]]

        x_dram = resid.rearrange("b (t p) d -> p (b t) d", p=P)
        out_dram = out.rearrange("b (t p) d -> p (b t) d", p=P)

        def walk(eng, step):
            for p in range(PEELED):
                step(0, p)
            with eng.Fori(0, B - 1) as b:
                for p in range(PEELED, NP):
                    step(b, p)
                for p in range(PEELED):
                    step(b + 1, p)
            for p in range(PEELED, NP):
                step(B - 1, p)

        def first(b, p, n):
            return isinstance(b, int) and b * NP + p < n

        def last(b, p):
            return isinstance(b, int) and b == B - 1 and p == NP - 1

        def last_b(b):
            return isinstance(b, int) and b == B - 1

        def before(b, p, n):
            return (b, p - n) if p >= n else (b - 1, p - n + NP)

        block = ctx.enter_context(nc.Block())

        @block.sync
        def _(sp):
            for b in (0, 2, 1, 3):
                sp.dma_start(x_res[:, b * TB:(b + 1) * TB, :], x_dram[:, b * TB:(b + 1) * TB, :]).then_inc(x_in, 16)
            row = lambda v: v.rearrange("(a d) -> a d", d=P)
            for at, src in ((C_LNG, row(ln_g)), (C_LNB, row(ln_b)), (C_ATTNB, row(attn_b)), (C_NEXTB, row(next_b)),
                            (C_ALNW, row(aln_w)), (C_ALNB, row(aln_b)), (C_B2, b2),
                            (C_B1, b1.rearrange("e (c d) -> (e c) d", d=P)),
                            (C_BQ, b_q.rearrange("(j t) e -> j (t e)", t=2)),
                            (C_BK, b_k.rearrange("(j t) e -> j (t e)", t=2))):
                sp.dma_start(const_rows[at:at + src.shape[0], :], src).then_inc(rows_in, 16)
            sp.dma_start(wattn[:], attn_w).then_inc(wdense_in, 16)
            sp.dma_start(wnext[:], next_w).then_inc(wdense_in, 16)

            def load_expert(f, e):
                if f * E + e >= NW:
                    sp.wait_ge(y_full, f * E + e - NW + 1)
                sp.dma_start(w1_sb[:, e % NW, :], w1[e]).then_inc(expert_in[e % NW], 16)
                sp.dma_start(w2_sb[:, e % NW, :, :], w2[e].rearrange("(c p) d -> p c d", p=P)
                             ).then_inc(expert_in[e % NW], 16)

            for e in range(NW):
                load_expert(0, e)
            for i, w in enumerate((W_q, W_k, W_v)):
                sp.dma_start(wproj[:, i, :].rearrange("p (h e) -> p h e", h=H),
                             w.rearrange("h d e -> d h e")).then_inc(wproj_in, 16)
            sp.dma_start(wo[:], W_o.rearrange("(j t) e d -> (t e) j d", t=2)).then_inc(wo_in, 16)
            sp.dma_start(bv_row[:], b_v.rearrange("(a h) e -> a (h e)", a=1).broadcast_to([P, H * DH])
                         ).then_inc(bv_in, 16)
            sp.dma_start(bo_row[:], row(b_o).broadcast_to([P, D])).then_inc(bo_in, 16)
            for e in range(NW, E):
                load_expert(0, e)

            def stage_x(b):
                for dst, src in ((xcur_hi, xT_hi), (xcur_lo, xT_lo)):
                    sp.dma_start(dst[:].bitcast(F32), src[:, bass.ds(b, 1), :].rearrange("p a s -> p (a s)").bitcast(F32)
                                 ).then_inc(xcur_in, 16)

            sp.wait_ge(xhi_ready, 1)
            sp.wait_ge(xlo_ready, 1)
            stage_x(0)
            for e in range(NW):
                load_expert(1, e)
            sp.wait_ge(xlo_ready, B)
            with sp.Fori(1, B) as b:
                sp.wait_ge(misc_free, b * 26 + (misc(0, 5, "v") + 1 - 26))
                stage_x(b)
            for e in range(NW, E):
                load_expert(1, e)
            for n, b in enumerate((0, 2, 1, 3)):
                sp.wait_ge(resid_done, B + n + 1)
                sp.dma_start(out_dram[:, b * TB:(b + 1) * TB, :], x_res[:, b * TB:(b + 1) * TB, :]).then_inc(out_done, 16)
            sp.wait_ge(out_done, 16 * B)

        @block.gpsimd
        def _(pool):
            pool.memset(ident[:], 0.0).then_inc(pool_init, 1)
            pool.memset(mask[:], 0.0).then_inc(pool_init, 1)
            pool.memset(half_pow[:], -0.5).then_inc(pool_init, 1)
            pool.wait_ge(pool_init, 3)
            pool.affine_select(out=ident[:], in_=ident[:], compare_op=ALU.not_equal, fill=1.0, base=0,
                               pattern=[[-1, P]], channel_multiplier=1).then_inc(ident_ready, 1)
            tri = mask[:, S - P:S]
            pool.affine_select(out=tri, in_=tri, compare_op=ALU.is_ge, fill=NEG, base=0,
                               pattern=[[-1, P]], channel_multiplier=1).then_inc(mask_ready, 1)

            def rstd(n, par):
                pool.wait_ge(var_ready, n + 1)
                pool.tensor_tensor(st_rstd[:, par, :], st_var[:, par, :], half_pow[:], ALU.pow).then_inc(rstd_ready, 1)

            for n in range(8):
                rstd(n, n % 2)
            pool.wait_ge(wproj_in, 48)
            for i in range(3):
                pool.tensor_copy(wproj_hi[:, i, :], wproj[:, i, :]).then_inc(wsplit_hi, 1)
            for i in range(3):
                pool.wait_ge(wsplit_hi, i + 1)
                pool.tensor_tensor(wproj_lo[:, i, :], wproj[:, i, :], wproj_hi[:, i, :],
                                   ALU.subtract).then_inc(wsplit_ready, 1)
            for n in range(8, 12):
                rstd(n, n % 2)

            def add_bo(b):
                pool.wait_ge(normed, TB * norms_up_to(1, b, 0))
                for t in range(b * TB, (b + 1) * TB):
                    pool.tensor_tensor(x_res[:, t, :], x_res[:, t, :], bo_row[:], ALU.add).then_inc(bo_added, 1)

            pool.wait_ge(bo_in, 16)

            def divide(g, p, half):
                pool.wait_ge(rec_ready, g * 2 + (half + 1))
                for s in range(4 * half, 4 * half + 4):
                    qi, h = TB - 1 - s // 2, s % 2
                    chunk = prob[:, p % 2, h, Q_AT[qi]:Q_AT[qi] + P * (qi + 1)]
                    pool.tensor_tensor(chunk, chunk, row_rec[:, p % 2, s:s + 1].broadcast_to([P, P * (qi + 1)]),
                                       ALU.mult).then_inc(prob_ready, 1)

            def step(b, p):
                g = b * NP + p
                if not first(b, p, 1):
                    divide(g - 1, p + 1, 1)
                if isinstance(b, int) and b == 0 and p < 2:
                    rstd(12 + 2 * p, 0)
                divide(g, p, 0)
                if isinstance(b, int) and b == 0 and p < 2:
                    rstd(13 + 2 * p, 1)
                    add_bo(2 * p + 1)
                    add_bo(2 * p)
                if p in (2, 3) and not first(b, p, NP):
                    rstd(b * 2 + (LOOP_NORMS - 2 + p - 2), p - 2)

            walk(pool, step)
            divide(G - 1, NP - 1, 1)
            rstd(LOOP_NORMS + 2 * B - 2, 0)
            rstd(LOOP_NORMS + 2 * B - 1, 1)

        @block.scalar
        def _(act):
            def norm_affine(f, k):
                for j, b in enumerate(PAIRS_OF_SEQUENCES[k]):
                    act.wait_ge(nT_full, 4 * f + 2 * k + j + 1)
                    act.activation(xT[:, b, :], N_BANK[j][:], ACT.Identity, scale=consts[:, C_LNG:C_LNG + 1],
                                   bias=consts[:, C_LNB:C_LNB + 1]).then_inc(nT_ready, 1)

            def ffn(f):
                def hidden(e):
                    par = e % 2
                    for c in range(FC):
                        if c % 2 == 0:
                            act.wait_ge(h_full, ((f * E + e) * FC + c) // 2 + 1)
                        act.activation(hT[:, par, c, :], H_BANK[par][c // 2][:, (c % 2) * 256:(c % 2) * 256 + 256],
                                       ACT.Gelu, bias=consts[:, C_B1 + e * FC + c:C_B1 + e * FC + c + 1]
                                       ).then_inc(h_ready, 1)

                def output(e):
                    k, i = e // TB, e % TB
                    act.wait_ge(y_full, f * E + e + 1)
                    act.activation(yT[:, k:k + 3:2, i * P:(i + 1) * P],
                                   Y_BANK[e % 2][:, 0:MB * P].rearrange("p (m t) -> p m t", m=MB), ACT.Identity,
                                   bias=consts[:, C_B2 + e:C_B2 + e + 1]).then_inc(y_ready, 1)

                def experts(k):
                    hidden(TB * k)
                    for e in range(TB * k, TB * k + TB):
                        if e + 1 < TB * k + TB:
                            hidden(e + 1)
                        output(e)

                def last_gelu(k):
                    for j in range(2):
                        n = 4 * f + 2 * k + j
                        act.wait_ge(next_full, n + 1)
                        if n >= 2:
                            act.wait_ge(oback_full, n - 1)
                        act.activation(oT[:, j, :], O_BANK[j][:], ACT.Gelu,
                                       bias=consts[:, C_NEXTB:C_NEXTB + 1]).then_inc(o_ready, 1)

                if f == 0:
                    norm_affine(0, 0)
                experts(0)
                norm_affine(f, 1)
                last_gelu(0)
                experts(1)
                if f == 0:
                    for j, b in enumerate((0, 2)):
                        act.wait_ge(xin_ready, j + 1)
                        high(b)
                last_gelu(1)

            def high(b):
                act.copy(xT_hi[:, b, :], xT[:, b, :]).then_inc(xhi_ready, 1)

            act.wait_ge(consts_T, 1)
            act.copy(consts[:], banks[7][:, 0:NCONST]).then_inc(consts_ready, 1)
            act.wait_ge(consts_ready, 1)
            ffn(0)

            def qk_high(use, hi, par, col):
                act.wait_ge(misc_full, use + 1)
                act.activation(hi[:, par, :], MISC[:], ACT.Identity, bias=consts[:, col:col + 1]).then_inc(qk_hi_ready, 1)

            def exp_chunk(g, p, s):
                qi, h = TB - 1 - s // 2, s % 2
                act.wait_ge(s_masked, g * CPP + s + 1)
                chunk = prob[:, p % 2, h, Q_AT[qi]:Q_AT[qi] + P * (qi + 1)]
                act.activation(chunk, chunk, ACT.Exp, bias=neg_max[:, p % 2, s:s + 1], scale=-1.0,
                               accum_out=row_sum[:, p % 2, s:s + 1]).then_inc(exp_done, 1)

            def evac_pt(b, p, k):
                g = b * NP + p
                act.wait_ge(pt_full[1], g * 3 + k // 2 + 1)
                h, c = k // 3, k % 3
                act.copy(probT[:, p % 2, h, PT_AT[c]:PT_AT[c] + PT_WIDTH[c]], PT[1][:, 0:PT_WIDTH[c]]).then_inc(pt_evac[1], 1)

            def evac_z(b, p):
                act.wait_ge(pv_done, b * NP + p + 1)
                if p == 0 and not first(b, p, NP):
                    act.wait_ge(misc_full, misc(b, 2, "out") + 1)
                act.copy(zT[:, p, :], ZT[:]).then_inc(z_ready, 1)

            def step(b, p):
                g = b * NP + p
                nxt, par = (p + 1) % NP, (p + 1) % 2
                before_1 = not first(b, p, 1)
                if not last(b, p):
                    qk_high(misc(b, p, "k"), k_hi, par, C_BK + nxt)
                exp_chunk(g, p, 0)
                exp_chunk(g, p, 1)
                exp_chunk(g, p, 2)
                if not last(b, p):
                    qk_high(misc(b, p, "q"), q_hi, par, C_BQ + nxt)
                if before_1:
                    evac_pt(*before(b, p, 1), 1)
                exp_chunk(g, p, 3)
                if before_1:
                    evac_pt(*before(b, p, 1), 3)
                if not first(b, p, 2):
                    evac_z(*before(b, p, 2))
                exp_chunk(g, p, 4)
                exp_chunk(g, p, 5)
                if before_1:
                    evac_pt(*before(b, p, 1), 5)
                exp_chunk(g, p, 6)
                exp_chunk(g, p, 7)
                if isinstance(b, int) and b == 0 and p < 2:
                    act.wait_ge(misc_free, misc(0, p, "x") + 1)
                    high(2 * p + 1)

            qk_high(2, k_hi, 0, C_BK)
            qk_high(3, q_hi, 0, C_BQ)
            walk(act, step)
            evac_z(B - 1, NP - 2)
            for k in (1, 3, 5):
                evac_pt(B - 1, NP - 1, k)
            norm_affine(1, 0)
            evac_z(B - 1, NP - 1)
            ffn(1)

        @block.vector
        def _(dve):
            def tile(x, b, t):
                if isinstance(b, int):
                    return x[:, b * TB + t, :]
                return x[:, bass.ds(b * TB + t, 1), :].rearrange("p a d -> p (a d)")

            def norm_stats(n, par, b, src):
                for t in range(TB):
                    dve.bn_stats(stats[:, par, t, :], tile(src, b, t)).then_inc(stats_done, 1)
                dve.wait_ge(stats_done, n * TB + TB)
                mean_e, m2_e, mean_o, m2_o = (stats[:, par, :, k] for k in (1, 2, 4, 5))
                total, diff, m2, mean, diff2, var4, var = (
                    x[:, par, :] for x in (st_sum, st_diff, st_m2, st_mean, st_diff2, st_var4, st_var))
                dve.tensor_tensor(total, mean_e, mean_o, ALU.add).then_inc(norm_math, 1)
                dve.tensor_tensor(diff, mean_e, mean_o, ALU.subtract).then_inc(norm_math, 1)
                dve.tensor_tensor(m2, m2_e, m2_o, ALU.add).then_inc(norm_math, 1)
                dve.wait_ge(norm_math, n * 6 + 2)
                dve.tensor_tensor(diff2, diff, diff, ALU.mult).then_inc(norm_math, 1)
                dve.tensor_scalar(mean, total, 0.5, None, ALU.mult).then_inc(norm_math, 1)
                dve.wait_ge(norm_math, n * 6 + 4)
                dve.scalar_tensor_tensor(var4, m2, 4.0 / D, diff2, ALU.mult, ALU.add).then_inc(norm_math, 1)
                dve.wait_ge(norm_math, n * 6 + 6)
                dve.tensor_scalar(var, var4, 0.25, EPS, ALU.mult, ALU.add).then_inc(var_ready, 1)

            def norm_apply(n, par, b, src, dst):
                dve.wait_ge(rstd_ready, n + 1)
                for t in range(TB):
                    dve.tensor_scalar(tile(dst, b, t), tile(src, b, t), st_mean[:, par, t:t + 1],
                                      st_rstd[:, par, t:t + 1], ALU.subtract, ALU.mult).then_inc(normed, 1)

            def norm_pair(n, pair):
                for j in range(2):
                    norm_stats(n + j, j, pair[j], x_res)
                for j in range(2):
                    norm_apply(n + j, j, pair[j], x_res, x_norm)
                    dve.wait_ge(normed, TB * (n + j + 1))
                    norm_stats(n + 2 + j, j, pair[j], x_norm)
                for j in range(2):
                    norm_apply(n + 2 + j, j, pair[j], x_norm, x_norm2)

            def front(f, k):
                for j, b in enumerate(PAIRS_OF_SEQUENCES[k]):
                    dve.wait_ge(x0T_full, 4 * f + 2 * k + j + 1)
                    dve.tensor_scalar(x0T[:, b, :], X0_BANK[j][:], consts[:, C_ATTNB:C_ATTNB + 1], None,
                                      ALU.add).then_inc(x0T_ready, 1)

            def front_add(f, k):
                for j, b in enumerate(PAIRS_OF_SEQUENCES[k]):
                    dve.wait_ge(attn_full, 4 * f + 2 * k + j + 1)
                    dve.wait_ge(x0T_ready, 4 * f + 2 * k + j + 1)
                    dve.tensor_tensor(x0T[:, b, :], N_BANK[j][:], x0T[:, b, :], ALU.add).then_inc(xattn_ready, 1)

            def residual(f, k):
                for j, b in enumerate(PAIRS_OF_SEQUENCES[k]):
                    dve.wait_ge(oback_full, 4 * f + 2 * k + j + 1)
                    tiles = x_res[:, b * TB:(b + 1) * TB, :].rearrange("p t d -> p (t d)")
                    dve.scalar_tensor_tensor(tiles, O_BANK[j][:], 0.5, tiles, ALU.mult, ALU.add).then_inc(resid_done, 1)

            def x_affine(b, bank):
                return dve.tensor_scalar(xT[:, b, :], bank[:], consts[:, C_ALNW:C_ALNW + 1],
                                         consts[:, C_ALNB:C_ALNB + 1], ALU.mult, ALU.add)

            def x_low(b, n):
                dve.wait_ge(xhi_ready, n)
                dve.tensor_tensor(xT_lo[:, b, :], xT[:, b, :], xT_hi[:, b, :], ALU.subtract).then_inc(xlo_ready, 1)

            dve.wait_ge(x_in, 16 * B)
            norm_pair(0, (0, 2))
            dve.wait_ge(consts_ready, 1)
            front(0, 0)
            front_add(0, 0)
            norm_pair(4, (1, 3))
            front(0, 1)
            front_add(0, 1)
            residual(0, 0)
            dve.wait_ge(resid_done, 2)
            norm_pair(8, (0, 2))
            for j, b in enumerate((0, 2)):
                dve.wait_ge(xin_full, j + 1)
                x_affine(b, banks[3 + j]).then_inc(xin_ready, 1)
            for j, b in enumerate((0, 2)):
                x_low(b, j + 1)
            residual(0, 1)
            dve.wait_ge(resid_done, B)

            dve.wait_ge(bv_in, 16)
            dve.wait_ge(mask_ready, 1)
            chunks_wanted = dve.alloc_register("chunks_wanted")
            dve.reg_mov(chunks_wanted, PEELED * CPP + 1)

            def evac_v(t, half, use):
                dve.wait_ge(misc_full, use + 1)
                cols = slice(half * 512, half * 512 + 512)
                dve.tensor_tensor(v_sb[:, t, cols], MISC[:], bv_row[:, cols], ALU.add).then_inc(misc_free, 1)

            def qk_low(count, lo, hi, par, col):
                dve.wait_ge(qk_hi_ready, count)
                dve.scalar_tensor_tensor(lo[:, par, :], MISC[:], consts[:, col:col + 1], hi[:, par, :],
                                         ALU.add, ALU.subtract).then_inc(misc_free, 1)

            def mask_max(b, p, s, *also):
                g = b * NP + p
                qi, h = TB - 1 - s // 2, s % 2
                w = P * (qi + 1)
                wanted = g * CPP + s + 1 if isinstance(g, int) else dve.snap(chunks_wanted)
                for other in also:
                    dve.wait_ge(*other)
                dve.wait_ge(s_full, wanted)
                if not isinstance(g, int):
                    dve.reg_add(chunks_wanted, chunks_wanted, 1)
                dve.tensor_tensor_reduce(prob[:, p % 2, h, Q_AT[qi]:Q_AT[qi] + w], SCORE[s % 4][:, 0:w],
                                         mask[:, S - w:S], -SCALE, BIG, ALU.add, ALU.min,
                                         neg_max[:, p % 2, s:s + 1]).then_inc(s_masked, 1)

            def reciprocals(g, p, half):
                dve.wait_ge(exp_done, g * CPP + (4 * half + 4))
                cols = slice(4 * half, 4 * half + 4)
                dve.reciprocal(row_rec[:, p % 2, cols], row_sum[:, p % 2, cols]).then_inc(rec_ready, 1)

            def evac_pt(b, p, k):
                g = b * NP + p
                dve.wait_ge(pt_full[0], g * 3 + k // 2 + 1)
                h, c = k // 3, k % 3
                dve.tensor_copy(probT[:, p % 2, h, PT_AT[c]:PT_AT[c] + PT_WIDTH[c]], PT[0][:, 0:PT_WIDTH[c]]
                                ).then_inc(pt_evac[0], 1)

            def add_out(b, half, use):
                dve.wait_ge(misc_full, use + 1)
                tiles = x_res[:, bass.ds(b * TB + half * 2, 2), :].rearrange("p t d -> p (t d)")
                dve.tensor_tensor(tiles, MISC[:, 0:2 * P], tiles, ALU.add).then_inc(misc_free, 1)

            def step(b, p):
                g = b * NP + p
                nxt, par = (p + 1) % NP, (p + 1) % 2
                if first(b, p, 3) and p == 2:
                    dve.wait_ge(bo_added, NT)
                peeled_start = isinstance(b, int) and b == 0 and p < 2
                norms = not first(b, p, NP)
                n = b * 2 + (LOOP_NORMS - 2)
                before_1 = not first(b, p, 1)
                if norms and p == 3:
                    norm_apply(n, 0, b - 1, x_res, x_norm)
                if before_1:
                    reciprocals(g - 1, par, 1)
                if norms and p == 2:
                    add_out(b - 1, 1, misc(b, 2, "out"))
                mask_max(b, p, 0)
                mask_max(b, p, 1)
                if not last(b, p):
                    qk_low(g * 2 + 3, k_lo, k_hi, par, C_BK + nxt)
                mask_max(b, p, 2)
                mask_max(b, p, 3)
                if peeled_start:
                    norm_stats(12 + 2 * p, 0, 2 * p + 1, x_res)
                mask_max(b, p, 4)
                mask_max(b, p, 5)
                if before_1:
                    evac_pt(*before(b, p, 1), 0)
                if not last(b, p):
                    qk_low(g * 2 + 4, q_lo, q_hi, par, C_BQ + nxt)
                if before_1:
                    evac_pt(*before(b, p, 1), 2)
                if peeled_start:
                    norm_apply(12 + 2 * p, 0, 2 * p + 1, x_res, x_norm)
                    dve.wait_ge(normed, TB * (13 + 2 * p))
                    norm_stats(13 + 2 * p, 1, 2 * p + 1, x_norm)
                also = []
                if norms and p == 2:
                    also = [(misc_free, misc(b, 2, "out") + 1)]
                if norms and p == 3:
                    also = [(normed, n * TB + TB)]
                mask_max(b, p, 6, *also)
                reciprocals(g, p % 2, 0)
                mask_max(b, p, 7)
                if norms and p == 4:
                    norm_apply(n + 1, 1, b - 1, x_norm, x_norm2)
                if norms and p == 2:
                    norm_stats(n, 0, b - 1, x_res)
                if not (last_b(b) and p >= 6):
                    half, t = (1, p - 2) if 2 <= p <= 5 else (0, (p - 6) % NP)
                    evac_v(t, half, misc(b, p, "v"))
                if before_1:
                    evac_pt(*before(b, p, 1), 4)
                if peeled_start:
                    norm_apply(13 + 2 * p, 1, 2 * p + 1, x_norm, x_norm2)
                    dve.wait_ge(misc_full, misc(0, p, "x") + 1)
                    x_affine(2 * p + 1, MISC).then_inc(misc_free, 1)
                    x_low(2 * p + 1, 3 + p)
                if norms and p == 1:
                    add_out(b - 1, 0, misc(b, 1, "out"))
                if norms and p == 3:
                    norm_stats(n + 1, 1, b - 1, x_norm)

            for t in range(2):
                evac_v(t, 0, t)
            qk_low(1, k_lo, k_hi, 0, C_BK)
            qk_low(2, q_lo, q_hi, 0, C_BQ)
            walk(dve, step)
            reciprocals(G - 1, (NP - 1) % 2, 1)
            for k in (0, 2, 4):
                evac_pt(B - 1, NP - 1, k)
            front(1, 0)
            front_add(1, 0)
            for half in range(2):
                add_out(B - 1, half, LAST_OUT + half)
            dve.wait_ge(misc_free, LAST_OUT + 2)

            n = LOOP_NORMS + 2 * B - 2
            norm_stats(n, 0, B - 1, x_res)
            norm_apply(n, 0, B - 1, x_res, x_norm)
            dve.wait_ge(normed, n * TB + TB)
            norm_stats(n + 1, 1, B - 1, x_norm)
            norm_apply(n + 1, 1, B - 1, x_norm, x_norm2)
            front(1, 1)
            front_add(1, 1)
            residual(1, 0)
            residual(1, 1)

        @block.tensor
        def _(pe):
            def split_matmul(out_ap, hi_w, lo_w, hi_x, lo_x):
                pe.matmul(out_ap, lo_w, hi_x, start=True, stop=False)
                pe.matmul(out_ap, hi_w, lo_x, start=False, stop=False)
                return pe.matmul(out_ap, hi_w, hi_x, start=False, stop=True)

            def transpose_tiles(bank, src):
                for t in range(TB):
                    ins = pe.transpose(bank[:, t * P:(t + 1) * P], src(t), ident[:])
                return ins

            def front_transposes(f, k):
                pair = PAIRS_OF_SEQUENCES[k]
                if k == 1:
                    pe.wait_ge(y_ready, f * E + TB)
                for which, bank, full in ((0, X0_BANK, x0T_full), (1, N_BANK, nT_full)):
                    src = (x_norm, x_norm2)[which]
                    for j, b in enumerate(pair):
                        pe.wait_ge(normed, TB * norms_up_to(2 * f, b, which))
                        transpose_tiles(bank[j], lambda t: src[:, b * TB + t, :]).then_inc(full, 1)

            def attn_dense(f, k):
                for j, b in enumerate(PAIRS_OF_SEQUENCES[k]):
                    pe.wait_ge(nT_ready, 4 * f + 2 * k + j + 1)
                    pe.matmul(N_BANK[j][:], wattn[:], xT[:, b, :], start=True, stop=True).then_inc(attn_full, 1)

            def hidden(f, e):
                par, k, i = e % 2, e // TB, e % TB
                pe.wait_ge(expert_in[e % NW], 32 * (f * E // NW + e // NW + 1))
                x_e = x0T[:, k:k + 3:2, i * P:(i + 1) * P]
                for c in range(FC):
                    ins = pe.matmul(H_BANK[par][c // 2][:, (c % 2) * 256:(c % 2) * 256 + 256].rearrange(
                        "p (m t) -> p m t", m=MB), w1_sb[:, e % NW, c * P:(c + 1) * P], x_e, start=True, stop=True)
                    if c % 2 == 1:
                        ins.then_inc(h_full, 1)

            def output(f, e):
                par = e % 2
                if e % TB >= 2:
                    pe.wait_ge(y_ready, f * E + e - 1)
                for c in range(FC):
                    pe.wait_ge(h_ready, (f * E + e) * FC + c + 1)
                    ins = pe.matmul(Y_BANK[par][:, 0:MB * P], w2_sb[:, e % NW, c, :], hT[:, par, c, :],
                                    start=(c == 0), stop=(c == FC - 1))
                ins.then_inc(y_full, 1)

            def experts(f, k):
                pe.wait_ge(xattn_ready, 4 * f + 2 * k + 2)
                hidden(f, TB * k)
                for e in range(TB * k, TB * k + TB):
                    if e + 1 < TB * k + TB:
                        if k == 1 and e == TB:
                            pe.wait_ge(resid_done, 4 * f + 2)
                        if f == 1 and e == 0:
                            pe.wait_ge(misc_free, LAST_OUT + 2)
                        hidden(f, e + 1)
                    output(f, e)

            def next_dense(f, k):
                pe.wait_ge(y_ready, f * E + TB * k + TB)
                for j, b in enumerate(PAIRS_OF_SEQUENCES[k]):
                    pe.matmul(O_BANK[j][:], wnext[:], yT[:, b, :], start=True, stop=True).then_inc(next_full, 1)

            def back(f, k):
                for j in range(2):
                    pe.wait_ge(o_ready, 4 * f + 2 * k + j + 1)
                    transpose_tiles(O_BANK[j], lambda t: oT[:, j, t * P:(t + 1) * P]).then_inc(oback_full, 1)

            def ffn_from_experts(f):
                experts(f, 0)
                front_transposes(f, 1)
                next_dense(f, 0)
                attn_dense(f, 1)
                back(f, 0)
                experts(f, 1)

            pe.wait_ge(ident_ready, 1)
            pe.wait_ge(rows_in, 16 * 10)
            pe.transpose(banks[7][:, 0:NCONST], const_rows[:], ident[0:NCONST, 0:NCONST]).then_inc(consts_T, 1)
            pe.wait_ge(consts_ready, 1)
            front_transposes(0, 0)
            pe.wait_ge(wdense_in, 32)
            attn_dense(0, 0)
            ffn_from_experts(0)
            for j, b in enumerate((0, 2)):
                pe.wait_ge(normed, TB * norms_up_to(1, b, 1))
                transpose_tiles(banks[3 + j], lambda t: x_norm2[:, b * TB + t, :]).then_inc(xin_full, 1)
            next_dense(0, 1)
            back(0, 1)

            def project_v(t, half, use):
                if use > 0 if isinstance(use, int) else True:
                    pe.wait_ge(misc_free, use)
                cols = slice(half * 512, half * 512 + 512)
                rows = slice(t * P, (t + 1) * P)
                split_matmul(MISC[:], xcur_hi[:, rows], xcur_lo[:, rows],
                             wproj_hi[:, 2, cols], wproj_lo[:, 2, cols]).then_inc(misc_full, 1)

            def project_qk(b, p, which, use):
                pe.wait_ge(misc_free, use)
                cols = slice(p * P, (p + 1) * P)
                x_hi, x_lo = (x[:, bass.ds(b, 1), :].rearrange("p a s -> p (a s)") for x in (xT_hi, xT_lo))
                split_matmul(MISC[:], wproj_hi[:, which, cols], wproj_lo[:, which, cols],
                             x_hi, x_lo).then_inc(misc_full, 1)

            def scores(b, p, qi):
                g = b * NP + p
                s = 2 * (TB - 1 - qi)
                if not (first(b, p, 1) and s < 4):
                    pe.wait_ge(s_masked, g * CPP + (s - 2))
                w = max(P * (qi + 1), 256)
                q = slice(qi * P, (qi + 1) * P)
                for n, (a, c) in enumerate(((q_lo, k_hi), (q_hi, k_lo), (q_hi, k_hi))):
                    for h in range(2):
                        rows = slice(h * DH, (h + 1) * DH)
                        ins = pe.matmul(SCORE[(s + h) % 4][:, 0:w], a[rows, p % 2, q], c[rows, p % 2, 0:w],
                                        start=(n == 0), stop=(n == 2))
                        if n == 2:
                            ins.then_inc(s_full, 1)

            def transposes(b, p, k):
                g = b * NP + p
                h, c = k // 3, k % 3
                pe.wait_ge(prob_ready, g * CPP + (7 if h == 0 else 8))
                if not (first(b, p, 1) and k < 2):
                    pe.wait_ge(pt_evac[k % 2], g * 3 + k // 2)
                for key, at in PT_CHUNKS[c]:
                    for qi in range(key, TB):
                        ins = pe.transpose(PT[k % 2][:, at + (qi - key) * P:at + (qi - key + 1) * P],
                                           prob[:, p % 2, h, Q_AT[qi] + key * P:Q_AT[qi] + (key + 1) * P], ident[:])
                ins.then_inc(pt_full[k % 2], 1)

            def times_v(b, p):
                g = b * NP + p
                for e in range(2):
                    pe.wait_ge(pt_evac[e], g * 3 + 3)
                if isinstance(g, int) and g > 0:
                    pe.wait_ge(z_ready, g)
                for key in range(TB):
                    w = S - key * P
                    for h in range(2):
                        cols = slice(p * P + h * DH, p * P + (h + 1) * DH)
                        ins = pe.matmul(ZT[h * DH:(h + 1) * DH, key * P:S], v_sb[:, key, cols],
                                        probT[:, p % 2, h, PT_OF_KEY[key]:PT_OF_KEY[key] + w],
                                        start=(key == 0), stop=(key == TB - 1))
                ins.then_inc(pv_done, 1)

            def out_proj(b, half, use):
                pe.wait_ge(misc_free, use)
                if half == 0:
                    pe.wait_ge(z_ready, b * NP + NP)
                for t in range(2):
                    tokens = slice((2 * half + t) * P, (2 * half + t + 1) * P)
                    for p in range(NP):
                        ins = pe.matmul(MISC[:, t * P:(t + 1) * P], zT[:, p, tokens], wo[:, p, :],
                                        start=(p == 0), stop=(p == NP - 1))
                ins.then_inc(misc_full, 1)

            def step(b, p):
                nb, nxt = (b, p + 1) if p + 1 < NP else (b + 1, 0)
                for k in range(2):
                    use = 2 + k if first(b, p, 1) else misc(*before(b, p, 1), "kq"[k])
                    pe.wait_ge(misc_free, use + 1)
                before_1 = not first(b, p, 1)
                scores(b, p, 3)
                if p == 2 and not first(b, p, NP):
                    out_proj(b - 1, 1, misc(b, p, "out"))
                scores(b, p, 2)
                if not last(b, p):
                    project_qk(nb, nxt, 1, misc(b, p, "k"))
                if not first(b, p, 2):
                    times_v(*before(b, p, 2))
                scores(b, p, 1)
                if not last(b, p):
                    project_qk(nb, nxt, 0, misc(b, p, "q"))
                if before_1:
                    transposes(*before(b, p, 1), 0)
                    transposes(*before(b, p, 1), 1)
                scores(b, p, 0)
                if before_1:
                    transposes(*before(b, p, 1), 2)
                    transposes(*before(b, p, 1), 3)
                if not (last_b(b) and p >= 6):
                    if p == 6:
                        pe.wait_ge(xcur_in, b * 32 + 64)
                    half, t = (1, p - 2) if 2 <= p <= 5 else (0, (p - 6) % NP)
                    project_v(t, half, misc(b, p, "v"))
                if before_1:
                    transposes(*before(b, p, 1), 4)
                    transposes(*before(b, p, 1), 5)
                if p == 1 and not first(b, p, NP):
                    out_proj(b - 1, 0, misc(b, p, "out"))
                if isinstance(b, int) and b == 0 and p < 2:
                    pe.wait_ge(normed, TB * norms_up_to(1, 2 * p + 1, 1))
                    pe.wait_ge(misc_free, misc(0, p, "x"))
                    transpose_tiles(MISC, lambda t: x_norm2[:, (2 * p + 1) * TB + t, :]).then_inc(misc_full, 1)

            pe.wait_ge(wsplit_ready, 3)
            pe.wait_ge(xcur_in, 32)
            pe.wait_ge(resid_done, B - 1)
            for t in range(2):
                project_v(t, 0, t)
            pe.wait_ge(wo_in, 16)
            project_qk(0, 0, 1, 2)
            project_qk(0, 0, 0, 3)
            walk(pe, step)
            times_v(B - 1, NP - 2)
            for k in range(6):
                transposes(B - 1, NP - 1, k)
            front_transposes(1, 0)
            times_v(B - 1, NP - 1)
            out_proj(B - 1, 0, LAST_OUT)
            attn_dense(1, 0)
            out_proj(B - 1, 1, LAST_OUT + 1)
            ffn_from_experts(1)
            next_dense(1, 1)
            back(1, 1)


_INS = ['L0_attn_resid_stream', 'L0_attn_W_q', 'L0_attn_W_k', 'L0_attn_W_v', 'L0_attn_W_o', 'L0_attn_b_q',
        'L0_attn_b_k', 'L0_attn_b_v', 'L0_attn_b_o', 'L0_attn_ln_w', 'L0_attn_ln_b', 'L0_ffn_ln_g', 'L0_ffn_ln_b',
        'L0_ffn_attn_w', 'L0_ffn_attn_b', 'L0_ffn_w1', 'L0_ffn_b1', 'L0_ffn_w2', 'L0_ffn_b2', 'L0_ffn_next_w',
        'L0_ffn_next_b']


def kernel(**inputs):
    import numpy as _np
    import concourse.bacc as _bacc
    from concourse import mybir as _mybir
    from concourse.bass_utils import run_bass_kernel_spmd as _run

    nc = _bacc.Bacc("TRN2", target_bir_lowering=False, num_devices=1)
    arrays, args = {}, []
    for name in _INS:
        a = _np.ascontiguousarray(inputs[name])
        arrays[f"in_{name}"] = a
        args.append(nc.dram_tensor(f"in_{name}", a.shape, _mybir.dt.from_np(a.dtype), kind="ExternalInput").ap())
    shape = inputs['L0_attn_resid_stream'].shape
    args.append(nc.dram_tensor("out_x", shape, _mybir.dt.float32, kind="ExternalOutput").ap())
    macaron_kernel(nc, *args)
    r = _run(nc, [arrays], core_ids=[0])
    return r.results[0]["out_x"]
```

```python
from contextlib import ExitStack

import concourse.bass as bass
from concourse import mybir

ALU = mybir.AluOpType
ACT = mybir.ActivationFunctionType
F32 = mybir.dt.float32
F32R = mybir.dt.float32r

P = 128
EPS = 1e-5
NEG = -1e30
BIG = 3e38


def macaron_kernel(nc, resid, W_q, W_k, W_v, W_o, b_q, b_k, b_v, b_o, aln_w, aln_b,
                   ln_g, ln_b, attn_w, attn_b, w1, b1, w2, b2, next_w, next_b, out):
    B, S, D = resid.shape
    H, _, DH = W_q.shape
    E, _, DFF = w1.shape
    NT = B * S // P
    TB = S // P
    FC = DFF // P
    NP = H // 2
    MB = NT // E
    G = B * NP
    SCALE = DH ** -0.5
    CPP = 2 * TB
    assert D == P and 2 * DH == P and S == 512 and MB == 2 and TB == 4 and NP == 8

    PT_CHUNKS = [[(0, 0)], [(1, 0), (3, 384)], [(2, 0)]]
    PT_WIDTH = [512, 512, 256]
    PT_AT = [0, 512, 1024]
    PT_OF_KEY = {0: 0, 1: 512, 3: 896, 2: 1024}
    Q_AT = [0, 128, 384, 768]
    HW = 1280
    NW = 4

    C_LNG, C_LNB, C_ATTNB, C_NEXTB, C_ALNW, C_ALNB = range(6)
    C_B2 = 6
    C_B1 = C_B2 + E
    C_BQ = C_B1 + E * FC
    C_BK = C_BQ + NP
    NCONST = C_BK + NP

    PEELED = 6
    PAIRS_OF_SEQUENCES = ((0, 2), (1, 3))

    def misc(b, p, what):
        if isinstance(b, int) and b == 0 and p < PEELED:
            return 2 + 3 * p + (p > 3) + ("k", "q", "v", "x").index(what)
        if p < 2:
            return b * 26 + (2 + 3 * p + ("k", "q", "v", "out").index(what))
        if p == 2:
            return b * 26 + (9 + ("out", "k", "q", "v").index(what))
        return b * 26 + (13 + 3 * (p - 3) + ("k", "q", "v").index(what))

    NORMS = [(b, which) for pair in PAIRS_OF_SEQUENCES for which in (0, 1) for b in pair]
    NORMS += [(0, 0), (2, 0), (0, 1), (2, 1), (1, 0), (1, 1), (3, 0), (3, 1)]
    LOOP_NORMS = len(NORMS)

    def norms_up_to(phase, b, which):
        if phase < 2:
            return NORMS.index((b, which), 8 * phase) + 1
        return LOOP_NORMS + 2 * b + which + 1

    with ExitStack() as ctx:
        def sb(name, shape, dt=F32):
            return ctx.enter_context(nc.sbuf_tensor(name, shape, dt))

        def sem(name):
            return ctx.enter_context(nc.semaphore(name))

        banks = [ctx.enter_context(nc.psum_tensor(f"bank{i}", [P, 512], F32)) for i in range(8)]

        ident = sb("ident", [P, P])
        mask = sb("mask", [P, S])
        const_rows = sb("const_rows", [NCONST, P])
        consts = sb("consts", [P, NCONST])
        table_loaded = sb("table_loaded", [P, 1])
        head_rows = sb("head_rows", [P, 2])
        half_pow = sb("half_pow", [P, TB])
        bv_row = sb("bv_row", [P, H * DH])
        bo_row = sb("bo_row", [P, D])
        wproj_hi = sb("wproj_hi", [P, 3, H * DH], F32R)
        wproj_lo = sb("wproj_lo", [P, 3, H * DH], F32R)
        wo = sb("wo", [P, NP, D])
        wattn = sb("wattn", [P, D])
        wnext = sb("wnext", [P, D])
        w1_sb = sb("w1_sb", [P, NW, DFF])
        w2_sb = sb("w2_sb", [P, NW, FC, D])

        x_res = sb("x_res", [P, NT, D])
        x_norm = sb("x_norm", [P, NT, D])
        x_norm2 = sb("x_norm2", [P, NT, D])
        stats = sb("stats", [P, 2, TB, 6])
        stats_seen = sb("stats_seen", [P, 1])
        mean_var = sb("mean_var", [P, 2, TB, 2])
        st_var = sb("st_var", [P, 2, TB])
        st_rstd = sb("st_rstd", [P, 2, TB])

        xT = sb("xT", [P, B, S])
        x0T = sb("x0T", [P, B, S])
        xT_hi = sb("xT_hi", [P, B, S], F32R)
        xT_lo = sb("xT_lo", [P, B, S], F32R)
        xcur_hi = sb("xcur_hi", [P, S], F32R)
        xcur_lo = sb("xcur_lo", [P, S], F32R)

        q_hi = sb("q_hi", [P, 2, S], F32R)
        q_lo = sb("q_lo", [P, 2, S], F32R)
        k_hi = sb("k_hi", [P, 2, S], F32R)
        k_lo = sb("k_lo", [P, 2, S], F32R)
        k0_hi = sb("k0_hi", [P, 2, 2 * P], F32R)
        k0_lo = sb("k0_lo", [P, 2, 2 * P], F32R)
        v_sb = sb("v_sb", [P, TB, H * DH])
        prob = sb("prob", [P, 2, 2, HW])
        probT = sb("probT", [P, 2, 2, HW])
        zT = sb("zT", [P, NP, S])
        wproj = probT[:].rearrange("p a b c -> p (a b c)")[:, 0:3 * H * DH].rearrange("p (i c) -> p i c", i=3)
        hT = prob[:].rearrange("p a b c -> p (a b c)")[:, 0:2 * FC * MB * P].rearrange("p (a c t) -> p a c t", a=2, c=FC)
        oT = zT[:, 0:2, :]
        yT = x_norm[:].rearrange("p (b t) d -> p b (t d)", b=B)
        neg_max = sb("neg_max", [P, 2, CPP])
        row_sum = sb("row_sum", [P, 2, CPP])
        row_rec = sb("row_rec", [P, 2, CPP])

        x_in = [sem(f"x_in{b}") for b in range(B)]
        rows_in = sem("rows_in")
        bv_in = sem("bv_in")
        bo_in = sem("bo_in")
        bo_added = sem("bo_added")
        wproj_in = sem("wproj_in")
        wo_in = sem("wo_in")
        wdense_in = sem("wdense_in")
        expert_in = [sem(f"expert_in{i}") for i in range(NW)]
        pool_init = sem("pool_init")
        ident_ready = sem("ident_ready")
        mask_ready = sem("mask_ready")
        wsplit_hi = sem("wsplit_hi")
        wsplit_ready = sem("wsplit_ready")
        consts_T = sem("consts_T")
        consts_ready = sem("consts_ready")
        stats_done = sem("stats_done")
        aggr_done = sem("aggr_done")
        var_ready = sem("var_ready")
        rstd_ready = sem("rstd_ready")
        normed = sem("normed")
        nT_full = sem("nT_full")
        x0T_full = sem("x0T_full")
        nT_ready = sem("nT_ready")
        x0T_ready = sem("x0T_ready")
        attn_full = sem("attn_full")
        xattn_ready = sem("xattn_ready")
        h_full = sem("h_full")
        h_ready = sem("h_ready")
        y_full = sem("y_full")
        y_ready = sem("y_ready")
        next_full = sem("next_full")
        o_ready = sem("o_ready")
        oback_full = sem("oback_full")
        resid_done = sem("resid_done")
        out_done = sem("out_done")
        v_first_full = sem("v_first_full")
        v_first_read = sem("v_first_read")
        last_out_full = sem("last_out_full")
        last_out_added = sem("last_out_added")
        xin_full = sem("xin_full")
        xin_ready = sem("xin_ready")
        xhi_ready = sem("xhi_ready")
        xlo_ready = sem("xlo_ready")
        xcur_in = sem("xcur_in")
        misc_full = sem("misc_full")
        misc_free = sem("misc_free")
        qk_hi_ready = sem("qk_hi_ready")
        head_rows_ready = sem("head_rows_ready")
        k0_ready = sem("k0_ready")
        s_full = sem("s_full")
        s_masked = sem("s_masked")
        exp_done = sem("exp_done")
        rec_ready = sem("rec_ready")
        prob_ready = sem("prob_ready")
        pt_full = [sem("pt_full0"), sem("pt_full1")]
        pt_evac = [sem("pt_evac0"), sem("pt_evac1")]
        pv_done = sem("pv_done")
        z_ready = sem("z_ready")

        MISC = banks[0]
        SCORE = banks[1:5]
        PT = banks[5:7]
        ZT = banks[7]
        X0_BANK = [banks[1], banks[3]]
        N_BANK = [banks[4], banks[2]]
        H_BANK = [banks[5:7], (banks[0], banks[7])]
        Y_BANK = [banks[1], banks[2]]
        O_BANK = [banks[0], banks[7]]

        x_dram = resid.rearrange("b (t p) d -> p (b t) d", p=P)
        out_dram = out.rearrange("b (t p) d -> p (b t) d", p=P)

        def walk(eng, step):
            for p in range(PEELED):
                step(0, p)
            with eng.Fori(0, B - 1) as b:
                for p in range(PEELED, NP):
                    step(b, p)
                for p in range(PEELED):
                    step(b + 1, p)
            for p in range(PEELED, NP):
                step(B - 1, p)

        def first(b, p, n):
            return isinstance(b, int) and b * NP + p < n

        def last(b, p):
            return isinstance(b, int) and b == B - 1 and p == NP - 1

        def last_b(b):
            return isinstance(b, int) and b == B - 1

        def before(b, p, n):
            return (b, p - n) if p >= n else (b - 1, p - n + NP)

        block = ctx.enter_context(nc.Block())

        @block.sync
        def _(sp):
            for b in (0, 2, 1, 3):
                sp.dma_start(x_res[:, b * TB:(b + 1) * TB, :], x_dram[:, b * TB:(b + 1) * TB, :]).then_inc(x_in[b], 16)
            row = lambda v: v.rearrange("(a d) -> a d", d=P)
            for at, src in ((C_LNG, row(ln_g)), (C_LNB, row(ln_b)), (C_ATTNB, row(attn_b)), (C_NEXTB, row(next_b)),
                            (C_ALNW, row(aln_w)), (C_ALNB, row(aln_b)), (C_B2, b2),
                            (C_B1, b1.rearrange("e (c d) -> (e c) d", d=P)),
                            (C_BQ, b_q.rearrange("(j t) e -> j (t e)", t=2)),
                            (C_BK, b_k.rearrange("(j t) e -> j (t e)", t=2))):
                sp.dma_start(const_rows[at:at + src.shape[0], :], src).then_inc(rows_in, 16)
            sp.dma_start(wattn[:], attn_w).then_inc(wdense_in, 16)
            sp.dma_start(wnext[:], next_w).then_inc(wdense_in, 16)

            def load_expert(f, e):
                if f * E + e >= NW:
                    sp.wait_ge(y_full, f * E + e - NW + 1)
                sp.dma_start(w1_sb[:, e % NW, :], w1[e]).then_inc(expert_in[e % NW], 16)
                sp.dma_start(w2_sb[:, e % NW, :, :], w2[e].rearrange("(c p) d -> p c d", p=P)
                             ).then_inc(expert_in[e % NW], 16)

            for e in range(NW):
                load_expert(0, e)
            for i, w in enumerate((W_q, W_k, W_v)):
                sp.dma_start(wproj[:, i, :].rearrange("p (h e) -> p h e", h=H),
                             w.rearrange("h d e -> d h e")).then_inc(wproj_in, 16)
            sp.dma_start(wo[:], W_o.rearrange("(j t) e d -> (t e) j d", t=2)).then_inc(wo_in, 16)
            sp.dma_start(bv_row[:], b_v.rearrange("(a h) e -> a (h e)", a=1).broadcast_to([P, H * DH])
                         ).then_inc(bv_in, 16)
            sp.dma_start(bo_row[:], row(b_o).broadcast_to([P, D])).then_inc(bo_in, 16)
            for e in range(NW, E):
                load_expert(0, e)

            def stage_x(b):
                for dst, src in ((xcur_hi, xT_hi), (xcur_lo, xT_lo)):
                    sp.dma_start(dst[:].bitcast(F32), src[:, bass.ds(b, 1), :].rearrange("p a s -> p (a s)").bitcast(F32)
                                 ).then_inc(xcur_in, 16)

            sp.wait_ge(xhi_ready, 1)
            sp.wait_ge(xlo_ready, 1)
            stage_x(0)
            for e in range(NW):
                load_expert(1, e)
            sp.wait_ge(xlo_ready, B)
            with sp.Fori(1, B) as b:
                sp.wait_ge(misc_free, b * 26 + (misc(0, 6, "k") - 26))
                stage_x(b)
            for e in range(NW, E):
                load_expert(1, e)
            for n, b in enumerate((0, 2, 1, 3)):
                sp.wait_ge(resid_done, B + n + 1)
                sp.dma_start(out_dram[:, b * TB:(b + 1) * TB, :], x_res[:, b * TB:(b + 1) * TB, :]).then_inc(out_done, 16)
            sp.wait_ge(out_done, 16 * B)

        @block.gpsimd
        def _(pool):
            pool.memset(ident[:], 0.0).then_inc(pool_init, 1)
            pool.memset(mask[:], 0.0).then_inc(pool_init, 1)
            pool.memset(half_pow[:], -0.5).then_inc(pool_init, 1)
            pool.memset(head_rows[:], 1.0).then_inc(pool_init, 1)
            pool.wait_ge(pool_init, 4)
            pool.affine_select(out=ident[:], in_=ident[:], compare_op=ALU.not_equal, fill=1.0, base=0,
                               pattern=[[-1, P]], channel_multiplier=1).then_inc(ident_ready, 1)
            tri = mask[:, S - P:S]
            pool.affine_select(out=tri, in_=tri, compare_op=ALU.is_ge, fill=NEG, base=0,
                               pattern=[[-1, P]], channel_multiplier=1).then_inc(mask_ready, 1)
            for h, (base, slope) in enumerate(((DH - 1, -1), (-DH, 1))):
                rows = head_rows[:, h:h + 1]
                pool.affine_select(out=rows, in_=rows, compare_op=ALU.is_ge, fill=0.0, base=base,
                                   pattern=[[0, 1]], channel_multiplier=slope).then_inc(head_rows_ready, 1)

            def rstd(n, par):
                pool.wait_ge(var_ready, n + 1)
                pool.tensor_tensor(st_rstd[:, par, :], st_var[:, par, :], half_pow[:], ALU.pow).then_inc(rstd_ready, 1)

            for n in range(8):
                rstd(n, n % 2)
            for i in range(3):
                pool.wait_ge(wsplit_hi, i + 1)
                pool.tensor_tensor(wproj_lo[:, i, :], wproj[:, i, :], wproj_hi[:, i, :],
                                   ALU.subtract).then_inc(wsplit_ready, 1)
            for n in range(8, 12):
                rstd(n, n % 2)

            def add_bo(b):
                pool.wait_ge(normed, TB * norms_up_to(1, b, 0))
                for t in range(b * TB, (b + 1) * TB):
                    pool.tensor_tensor(x_res[:, t, :], x_res[:, t, :], bo_row[:], ALU.add).then_inc(bo_added, 1)

            pool.wait_ge(bo_in, 16)
            add_bo(0)
            add_bo(2)

            def first_keys(use, par):
                pool.wait_ge(misc_free, use + 1)
                for k0, k in ((k0_hi, k_hi), (k0_lo, k_lo)):
                    pool.tensor_tensor(k0[:, par, :].rearrange("p (h t) -> p h t", h=2),
                                       k[:, par:par + 1, 0:P].broadcast_to([P, 2, P]),
                                       head_rows[:].rearrange("p (h a) -> p h a", a=1).broadcast_to([P, 2, P]),
                                       ALU.mult).then_inc(k0_ready, 1)

            def divide(g, p, half):
                pool.wait_ge(rec_ready, g * 2 + (half + 1))
                for s in range(4 * half, 4 * half + 4):
                    qi, h = TB - 1 - s // 2, s % 2
                    chunk = prob[:, p % 2, h, Q_AT[qi]:Q_AT[qi] + P * (qi + 1)]
                    pool.tensor_tensor(chunk, chunk, row_rec[:, p % 2, s:s + 1].broadcast_to([P, P * (qi + 1)]),
                                       ALU.mult).then_inc(prob_ready, 1)

            def step(b, p):
                g = b * NP + p
                if not first(b, p, 1):
                    divide(g - 1, p + 1, 1)
                if not last(b, p):
                    first_keys(misc(b, p, "k"), (p + 1) % 2)
                if first(b, p, PEELED) and p in (2, 4):
                    add_bo(p - 1)
                divide(g, p, 0)
                if first(b, p, 4):
                    rstd(12 + p, p % 2)
                if p in (2, 3) and not first(b, p, NP):
                    rstd(b * 2 + (LOOP_NORMS - 2 + p - 2), p - 2)

            pool.wait_ge(head_rows_ready, 2)
            first_keys(0, 0)
            walk(pool, step)
            divide(G - 1, NP - 1, 1)
            rstd(LOOP_NORMS + 2 * B - 2, 0)
            rstd(LOOP_NORMS + 2 * B - 1, 1)

        @block.scalar
        def _(act):
            def norm_affine_one(f, k, j):
                act.wait_ge(nT_full, 4 * f + 2 * k + j + 1)
                act.activation(xT[:, PAIRS_OF_SEQUENCES[k][j], :], N_BANK[j][:], ACT.Identity,
                               scale=consts[:, C_LNG:C_LNG + 1], bias=consts[:, C_LNB:C_LNB + 1]
                               ).then_inc(nT_ready, 1)

            def norm_affine(f, k):
                for j in range(2):
                    norm_affine_one(f, k, j)

            def ffn(f):
                def hidden(e):
                    par = e % 2
                    for c in range(FC):
                        if c % 2 == 0:
                            act.wait_ge(h_full, ((f * E + e) * FC + c) // 2 + 1)
                        act.activation(hT[:, par, c, :], H_BANK[par][c // 2][:, (c % 2) * 256:(c % 2) * 256 + 256],
                                       ACT.Gelu, bias=consts[:, C_B1 + e * FC + c:C_B1 + e * FC + c + 1]
                                       ).then_inc(h_ready, 1)

                def output(e):
                    k, i = e // TB, e % TB
                    act.wait_ge(y_full, f * E + e + 1)
                    act.activation(yT[:, k:k + 3:2, i * P:(i + 1) * P],
                                   Y_BANK[e % 2][:, 0:MB * P].rearrange("p (m t) -> p m t", m=MB), ACT.Identity,
                                   bias=consts[:, C_B2 + e:C_B2 + e + 1]).then_inc(y_ready, 1)

                def experts(k):
                    hidden(TB * k)
                    for e in range(TB * k, TB * k + TB):
                        if e + 1 < TB * k + TB:
                            hidden(e + 1)
                        if f == 0 and e == E - 1:
                            act.wait_ge(xin_ready, 1)
                            high(0)
                        output(e)
                        if f == 0 and k == 0 and e < 3:
                            act.wait_ge(wproj_in, 48)
                            act.copy(wproj_hi[:, e, :], wproj[:, e, :]).then_inc(wsplit_hi, 1)

                def last_gelu(k):
                    if f == 0 and k == 1:
                        qk_high(0, k_hi, 0, C_BK, banks[4])
                    for j in range(2):
                        n = 4 * f + 2 * k + j
                        act.wait_ge(next_full, n + 1)
                        if n >= 2:
                            act.wait_ge(oback_full, n - 1)
                        act.activation(oT[:, j, :], O_BANK[j][:], ACT.Gelu,
                                       bias=consts[:, C_NEXTB:C_NEXTB + 1]).then_inc(o_ready, 1)

                if f == 0:
                    norm_affine(0, 0)
                experts(0)
                norm_affine(f, 1)
                last_gelu(0)
                experts(1)
                last_gelu(1)
                if f == 0:
                    qk_high(1, q_hi, 0, C_BQ, banks[5])
                    load_table(ACT.Exp)
                    act.wait_ge(xin_ready, 2)
                    high(2)

            def load_table(func):
                act.activation(table_loaded[:], consts[:, 0:1], func)

            def high(b):
                act.copy(xT_hi[:, b, :], xT[:, b, :]).then_inc(xhi_ready, 1)

            def qk_high(use, hi, par, col, bank=MISC):
                act.wait_ge(misc_full, use + 1)
                act.activation(hi[:, par, :], bank[:], ACT.Identity, bias=consts[:, col:col + 1]).then_inc(qk_hi_ready, 1)

            act.wait_ge(consts_T, 1)
            act.copy(consts[:], banks[7][:, 0:NCONST]).then_inc(consts_ready, 1)
            act.wait_ge(consts_ready, 1)
            ffn(0)

            def exp_chunk(g, p, s):
                qi, h = TB - 1 - s // 2, s % 2
                act.wait_ge(s_masked, g * CPP + s + 1)
                chunk = prob[:, p % 2, h, Q_AT[qi]:Q_AT[qi] + P * (qi + 1)]
                act.activation(chunk, chunk, ACT.Exp, bias=neg_max[:, p % 2, s:s + 1], scale=-1.0,
                               accum_out=row_sum[:, p % 2, s:s + 1]).then_inc(exp_done, 1)

            def evac_pt(b, p, k):
                g = b * NP + p
                act.wait_ge(pt_full[1], g * 3 + k // 2 + 1)
                h, c = k // 3, k % 3
                act.copy(probT[:, p % 2, h, PT_AT[c]:PT_AT[c] + PT_WIDTH[c]], PT[1][:, 0:PT_WIDTH[c]]).then_inc(pt_evac[1], 1)

            def evac_z(b, p):
                act.wait_ge(pv_done, b * NP + p + 1)
                if p == 0 and not first(b, p, NP):
                    act.wait_ge(misc_full, misc(b, 2, "out") + 1)
                act.copy(zT[:, p, :], ZT[:]).then_inc(z_ready, 1)

            def step(b, p):
                g = b * NP + p
                nxt, par = (p + 1) % NP, (p + 1) % 2
                before_1 = not first(b, p, 1)
                if not last(b, p):
                    qk_high(misc(b, p, "k"), k_hi, par, C_BK + nxt)
                exp_chunk(g, p, 0)
                exp_chunk(g, p, 1)
                exp_chunk(g, p, 2)
                if not last(b, p):
                    qk_high(misc(b, p, "q"), q_hi, par, C_BQ + nxt)
                if before_1:
                    evac_pt(*before(b, p, 1), 1)
                exp_chunk(g, p, 3)
                if before_1:
                    evac_pt(*before(b, p, 1), 3)
                if not first(b, p, 2):
                    evac_z(*before(b, p, 2))
                for s in range(4, CPP):
                    exp_chunk(g, p, s)
                if before_1:
                    evac_pt(*before(b, p, 1), 5)
                if first(b, p, PEELED) and p in (3, 5):
                    act.wait_ge(misc_free, misc(0, p, "x") + 1)
                    high(p - 2)

            walk(act, step)
            load_table(ACT.Gelu)
            norm_affine_one(1, 0, 0)
            evac_z(B - 1, NP - 2)
            evac_pt(B - 1, NP - 1, 1)
            norm_affine_one(1, 0, 1)
            evac_pt(B - 1, NP - 1, 3)
            evac_pt(B - 1, NP - 1, 5)
            evac_z(B - 1, NP - 1)
            ffn(1)

        @block.vector
        def _(dve):
            chunks_wanted = dve.alloc_register("chunks_wanted")

            def tile(x, b, t):
                if isinstance(b, int):
                    return x[:, b * TB + t, :]
                return x[:, bass.ds(b * TB + t, 1), :].rearrange("p a d -> p (a d)")

            def norm_stats(n, par, b, src):
                for t in range(TB):
                    dve.bn_stats(stats[:, par, t, :], tile(src, b, t)).then_inc(stats_done, 1)
                dve.wait_ge(stats_done, n * TB + TB)
                if not isinstance(n, int):
                    dve.tensor_copy(stats_seen[:], stats[:, par, 0, 0:1])
                for t in range(TB):
                    dve.bn_aggr(mean_var[:, par, t, :], stats[:, par, t, :]).then_inc(aggr_done, 1)
                dve.wait_ge(aggr_done, n * TB + TB)
                dve.tensor_scalar(st_var[:, par, :], mean_var[:, par, :, 1], EPS, None, ALU.add).then_inc(var_ready, 1)

            def norm_apply(n, par, b, src, dst):
                dve.wait_ge(rstd_ready, n + 1)
                for t in range(TB):
                    dve.tensor_scalar(tile(dst, b, t), tile(src, b, t), mean_var[:, par, t, 0:1],
                                      st_rstd[:, par, t:t + 1], ALU.subtract, ALU.mult).then_inc(normed, 1)

            def norm_pair(n, pair):
                for j in range(2):
                    if n < 8:
                        dve.wait_ge(x_in[pair[j]], 16)
                    norm_stats(n + j, j, pair[j], x_res)
                for j in range(2):
                    norm_apply(n + j, j, pair[j], x_res, x_norm)
                    dve.wait_ge(normed, TB * (n + j + 1))
                    norm_stats(n + 2 + j, j, pair[j], x_norm)
                for j in range(2):
                    norm_apply(n + 2 + j, j, pair[j], x_norm, x_norm2)

            def front_one(f, k, j):
                dve.wait_ge(x0T_full, 4 * f + 2 * k + j + 1)
                dve.tensor_scalar(x0T[:, PAIRS_OF_SEQUENCES[k][j], :], X0_BANK[j][:], consts[:, C_ATTNB:C_ATTNB + 1],
                                  None, ALU.add).then_inc(x0T_ready, 1)

            def front(f, k):
                for j in range(2):
                    front_one(f, k, j)

            def front_add(f, k):
                for j, b in enumerate(PAIRS_OF_SEQUENCES[k]):
                    dve.wait_ge(attn_full, 4 * f + 2 * k + j + 1)
                    dve.wait_ge(x0T_ready, 4 * f + 2 * k + j + 1)
                    dve.tensor_tensor(x0T[:, b, :], N_BANK[j][:], x0T[:, b, :], ALU.add).then_inc(xattn_ready, 1)

            def residual(f, k):
                for j, b in enumerate(PAIRS_OF_SEQUENCES[k]):
                    dve.wait_ge(oback_full, 4 * f + 2 * k + j + 1)
                    tiles = x_res[:, b * TB:(b + 1) * TB, :].rearrange("p t d -> p (t d)")
                    dve.scalar_tensor_tensor(tiles, O_BANK[j][:], 0.5, tiles, ALU.mult, ALU.add).then_inc(resid_done, 1)

            def x_affine(b, bank):
                return dve.tensor_scalar(xT[:, b, :], bank[:], consts[:, C_ALNW:C_ALNW + 1],
                                         consts[:, C_ALNB:C_ALNB + 1], ALU.mult, ALU.add)

            def x_low(b, n):
                dve.wait_ge(xhi_ready, n)
                dve.tensor_tensor(xT_lo[:, b, :], xT[:, b, :], xT_hi[:, b, :], ALU.subtract).then_inc(xlo_ready, 1)

            def qk_low(count, lo, hi, par, col, bank=MISC):
                dve.wait_ge(qk_hi_ready, count)
                dve.scalar_tensor_tensor(lo[:, par, :], bank[:], consts[:, col:col + 1], hi[:, par, :],
                                         ALU.add, ALU.subtract).then_inc(misc_free, 1)

            norm_pair(0, (0, 2))
            dve.wait_ge(consts_ready, 1)
            front(0, 0)
            front_add(0, 0)
            norm_pair(4, (1, 3))
            front(0, 1)
            front_add(0, 1)
            residual(0, 0)
            dve.wait_ge(resid_done, 2)
            norm_stats(8, 0, 0, x_res)
            norm_stats(9, 1, 2, x_res)
            norm_apply(8, 0, 0, x_res, x_norm)
            dve.wait_ge(normed, TB * 9)
            norm_stats(10, 0, 0, x_norm)
            norm_apply(9, 1, 2, x_res, x_norm)
            norm_apply(10, 0, 0, x_norm, x_norm2)
            dve.wait_ge(normed, TB * 10)
            norm_stats(11, 1, 2, x_norm)
            dve.wait_ge(xin_full, 1)
            x_affine(0, banks[3]).then_inc(xin_ready, 1)
            x_low(0, 1)
            norm_apply(11, 1, 2, x_norm, x_norm2)
            qk_low(1, k_lo, k_hi, 0, C_BK, banks[4])
            qk_low(2, q_lo, q_hi, 0, C_BQ, banks[5])
            residual(0, 1)
            dve.wait_ge(xin_full, 2)
            x_affine(2, banks[6]).then_inc(xin_ready, 1)
            x_low(2, 2)
            dve.wait_ge(resid_done, B)
            dve.wait_ge(bv_in, 16)
            dve.wait_ge(mask_ready, 1)
            dve.reg_mov(chunks_wanted, PEELED * CPP + 1)

            def evac_v(t, half, use):
                dve.wait_ge(misc_full, use + 1)
                cols = slice(half * 512, half * 512 + 512)
                dve.tensor_tensor(v_sb[:, t, cols], MISC[:], bv_row[:, cols], ALU.add).then_inc(misc_free, 1)

            def evac_first_v(t):
                dve.wait_ge(v_first_full, t + 1)
                dve.tensor_tensor(v_sb[:, t, 0:512], ZT[:], bv_row[:, 0:512], ALU.add).then_inc(v_first_read, 1)

            def mask_max(b, p, s):
                g = b * NP + p
                qi, h = TB - 1 - s // 2, s % 2
                w = P * (qi + 1)
                wanted = g * CPP + s + 1 if isinstance(g, int) else dve.snap(chunks_wanted)
                dve.wait_ge(s_full, wanted)
                if not isinstance(g, int):
                    dve.reg_add(chunks_wanted, chunks_wanted, 1)
                src = SCORE[s % 4][:, 0:w] if qi > 0 else SCORE[2][:, h * P:(h + 1) * P]
                dve.tensor_tensor_reduce(prob[:, p % 2, h, Q_AT[qi]:Q_AT[qi] + w], src,
                                         mask[:, S - w:S], -SCALE, BIG, ALU.add, ALU.min,
                                         neg_max[:, p % 2, s:s + 1]).then_inc(s_masked, 1)

            def reciprocals(g, p, half):
                dve.wait_ge(exp_done, g * CPP + (4 * half + 4))
                cols = slice(4 * half, 4 * half + 4)
                dve.reciprocal(row_rec[:, p % 2, cols], row_sum[:, p % 2, cols]).then_inc(rec_ready, 1)

            def evac_pt(b, p, k):
                g = b * NP + p
                dve.wait_ge(pt_full[0], g * 3 + k // 2 + 1)
                h, c = k // 3, k % 3
                dve.tensor_copy(probT[:, p % 2, h, PT_AT[c]:PT_AT[c] + PT_WIDTH[c]], PT[0][:, 0:PT_WIDTH[c]]
                                ).then_inc(pt_evac[0], 1)

            def add_out(b, half, use):
                dve.wait_ge(misc_full, use + 1)
                tiles = x_res[:, bass.ds(b * TB + half * 2, 2), :].rearrange("p t d -> p (t d)")
                dve.tensor_tensor(tiles, MISC[:, 0:2 * P], tiles, ALU.add).then_inc(misc_free, 1)

            def step(b, p):
                g = b * NP + p
                nxt, par = (p + 1) % NP, (p + 1) % 2
                after_first = not first(b, p, NP)
                first_stats = middle = last_apply = None
                if after_first and 2 <= p <= 4:
                    norm = (b * 2 + (LOOP_NORMS - 2), b - 1)
                    first_stats, middle, last_apply = (norm if p == at else None for at in (2, 3, 4))
                if first(b, p, PEELED):
                    first_stats = {0: (12, 1), 2: (14, 3)}.get(p)
                    middle = {1: (12, 1), 3: (14, 3)}.get(p)
                    last_apply = {2: (12, 1), 4: (14, 3)}.get(p)
                before_1 = not first(b, p, 1)
                if before_1:
                    reciprocals(g - 1, par, 1)
                if after_first and p == 2:
                    add_out(b - 1, 1, misc(b, 2, "out"))
                mask_max(b, p, 0)
                mask_max(b, p, 1)
                if not last(b, p):
                    qk_low(g * 2 + 3, k_lo, k_hi, par, C_BK + nxt)
                mask_max(b, p, 2)
                mask_max(b, p, 3)
                if first(b, p, 2):
                    evac_first_v(p)
                if middle:
                    norm_apply(middle[0], 0, middle[1], x_res, x_norm)
                if before_1:
                    evac_pt(*before(b, p, 1), 0)
                if not last(b, p):
                    qk_low(g * 2 + 4, q_lo, q_hi, par, C_BQ + nxt)
                if before_1:
                    evac_pt(*before(b, p, 1), 2)
                reciprocals(g, p % 2, 0)
                mask_max(b, p, 4)
                mask_max(b, p, 5)
                mask_max(b, p, 6)
                if not (last_b(b) and p >= 6):
                    half, t = (1, p - 2) if 2 <= p <= 5 else (0, (p - 6) % NP)
                    evac_v(t, half, misc(b, p, "v"))
                mask_max(b, p, 7)
                if after_first and p == 1:
                    add_out(b - 1, 0, misc(b, 1, "out"))
                if after_first and first_stats:
                    dve.wait_ge(misc_free, misc(b, 2, "out") + 1)
                if middle:
                    dve.wait_ge(normed, middle[0] * TB + TB)
                if before_1:
                    evac_pt(*before(b, p, 1), 4)
                if last_apply:
                    norm_apply(last_apply[0] + 1, 1, last_apply[1], x_norm, x_norm2)
                if first(b, p, PEELED) and p in (3, 5):
                    dve.wait_ge(misc_full, misc(0, p, "x") + 1)
                    x_affine(p - 2, MISC).then_inc(misc_free, 1)
                    x_low(p - 2, 2 + p // 2)
                if first(b, p, PEELED) and p == 5:
                    dve.wait_ge(bo_added, NT)
                if middle:
                    norm_stats(middle[0] + 1, 1, middle[1], x_norm)
                if first_stats:
                    norm_stats(first_stats[0], 0, first_stats[1], x_res)

            walk(dve, step)
            reciprocals(G - 1, (NP - 1) % 2, 1)
            front_one(1, 0, 0)
            evac_pt(B - 1, NP - 1, 0)
            front_one(1, 0, 1)
            evac_pt(B - 1, NP - 1, 2)
            evac_pt(B - 1, NP - 1, 4)
            front_add(1, 0)
            dve.wait_ge(last_out_full, 1)
            tiles = x_res[:, (B - 1) * TB:B * TB, :].rearrange("p t d -> p (t d)")
            dve.tensor_tensor(tiles, banks[3][:], tiles, ALU.add).then_inc(last_out_added, 1)
            dve.wait_ge(last_out_added, 1)

            n = LOOP_NORMS + 2 * B - 2
            norm_stats(n, 0, B - 1, x_res)
            norm_apply(n, 0, B - 1, x_res, x_norm)
            dve.wait_ge(normed, n * TB + TB)
            norm_stats(n + 1, 1, B - 1, x_norm)
            norm_apply(n + 1, 1, B - 1, x_norm, x_norm2)
            front(1, 1)
            front_add(1, 1)
            residual(1, 0)
            residual(1, 1)

        @block.tensor
        def _(pe):
            def split_matmul(out_ap, hi_w, lo_w, hi_x, lo_x):
                pe.matmul(out_ap, lo_w, hi_x, start=True, stop=False)
                pe.matmul(out_ap, hi_w, lo_x, start=False, stop=False)
                return pe.matmul(out_ap, hi_w, hi_x, start=False, stop=True)

            def transpose_tiles(bank, src):
                for t in range(TB):
                    ins = pe.transpose(bank[:, t * P:(t + 1) * P], src(t), ident[:])
                return ins

            def front_transpose(f, k, which, j):
                src, bank, full = ((x_norm, X0_BANK, x0T_full), (x_norm2, N_BANK, nT_full))[which]
                b = PAIRS_OF_SEQUENCES[k][j]
                pe.wait_ge(normed, TB * norms_up_to(2 * f, b, which))
                transpose_tiles(bank[j], lambda t: src[:, b * TB + t, :]).then_inc(full, 1)

            def front_transposes(f, k):
                if f == 1 and k == 1:
                    pe.wait_ge(last_out_added, 1)
                for which in (0, 1):
                    for j in range(2):
                        if k == 1 and (which, j) in ((0, 0), (1, 1)):
                            pe.wait_ge(y_ready, f * E + TB - 1 + j)
                        front_transpose(f, k, which, j)

            def attn_dense(f, k):
                for j, b in enumerate(PAIRS_OF_SEQUENCES[k]):
                    pe.wait_ge(nT_ready, 4 * f + 2 * k + j + 1)
                    pe.matmul(N_BANK[j][:], wattn[:], xT[:, b, :], start=True, stop=True).then_inc(attn_full, 1)

            def hidden(f, e):
                par, k, i = e % 2, e // TB, e % TB
                pe.wait_ge(expert_in[e % NW], 32 * (f * E // NW + e // NW + 1))
                x_e = x0T[:, k:k + 3:2, i * P:(i + 1) * P]
                for c in range(FC):
                    ins = pe.matmul(H_BANK[par][c // 2][:, (c % 2) * 256:(c % 2) * 256 + 256].rearrange(
                        "p (m t) -> p m t", m=MB), w1_sb[:, e % NW, c * P:(c + 1) * P], x_e, start=True, stop=True)
                    if c % 2 == 1:
                        ins.then_inc(h_full, 1)

            def output(f, e):
                par = e % 2
                if e % TB >= 2:
                    pe.wait_ge(y_ready, f * E + e - 1)
                for c in range(FC):
                    pe.wait_ge(h_ready, (f * E + e) * FC + c + 1)
                    ins = pe.matmul(Y_BANK[par][:, 0:MB * P], w2_sb[:, e % NW, c, :], hT[:, par, c, :],
                                    start=(c == 0), stop=(c == FC - 1))
                ins.then_inc(y_full, 1)

            def experts(f, k):
                pe.wait_ge(xattn_ready, 4 * f + 2 * k + 2)
                hidden(f, TB * k)
                for e in range(TB * k, TB * k + TB):
                    if e + 1 < TB * k + TB:
                        if k == 1 and e == TB:
                            pe.wait_ge(resid_done, 4 * f + 2)
                        if f == 1 and e == 0:
                            pe.wait_ge(z_ready, G)
                            pe.wait_ge(x0T_ready, 4 * f + 2)
                            out_proj(range(TB), banks[3]).then_inc(last_out_full, 1)
                        hidden(f, e + 1)
                    if f == 0 and e == E - 2:
                        pe.wait_ge(normed, TB * norms_up_to(1, 0, 1))
                        transpose_tiles(banks[3], lambda t: x_norm2[:, t, :]).then_inc(xin_full, 1)
                    output(f, e)

            def next_dense(f, k):
                pe.wait_ge(y_ready, f * E + TB * k + TB)
                for j, b in enumerate(PAIRS_OF_SEQUENCES[k]):
                    pe.matmul(O_BANK[j][:], wnext[:], yT[:, b, :], start=True, stop=True).then_inc(next_full, 1)

            def back(f, k):
                for j in range(2):
                    pe.wait_ge(o_ready, 4 * f + 2 * k + j + 1)
                    transpose_tiles(O_BANK[j], lambda t: oT[:, j, t * P:(t + 1) * P]).then_inc(oback_full, 1)

            def ffn_from_experts(f):
                experts(f, 0)
                front_transposes(f, 1)
                next_dense(f, 0)
                attn_dense(f, 1)
                back(f, 0)
                experts(f, 1)

            def project_v(t, half, bank=MISC):
                cols = slice(half * 512, half * 512 + 512)
                rows = slice(t * P, (t + 1) * P)
                return split_matmul(bank[:], xcur_hi[:, rows], xcur_lo[:, rows],
                                    wproj_hi[:, 2, cols], wproj_lo[:, 2, cols])

            def project_qk(b, p, which, use, bank=MISC):
                if use is not None:
                    pe.wait_ge(misc_free, use)
                cols = slice(p * P, (p + 1) * P)
                x_hi, x_lo = (x[:, bass.ds(b, 1), :].rearrange("p a s -> p (a s)") for x in (xT_hi, xT_lo))
                split_matmul(bank[:], wproj_hi[:, which, cols], wproj_lo[:, which, cols],
                             x_hi, x_lo).then_inc(misc_full, 1)

            def scores(b, p, qi):
                g = b * NP + p
                s = 2 * (TB - 1 - qi)
                if not (first(b, p, 1) and s < 4):
                    pe.wait_ge(s_masked, g * CPP + (s - 2))
                w = P * (qi + 1)
                q = slice(qi * P, (qi + 1) * P)
                if qi == 0:
                    pe.wait_ge(k0_ready, g * 2 + 2)
                    split_matmul(SCORE[2][:, 0:2 * P], q_hi[:, p % 2, q], q_lo[:, p % 2, q],
                                 k0_hi[:, p % 2, :], k0_lo[:, p % 2, :]).then_inc(s_full, 2)
                    return
                for n, (a, c) in enumerate(((q_lo, k_hi), (q_hi, k_lo), (q_hi, k_hi))):
                    for h in range(2):
                        rows = slice(h * DH, (h + 1) * DH)
                        ins = pe.matmul(SCORE[(s + h) % 4][:, 0:w], a[rows, p % 2, q], c[rows, p % 2, 0:w],
                                        start=(n == 0), stop=(n == 2))
                        if n == 2:
                            ins.then_inc(s_full, 1)

            def transposes(b, p, k):
                g = b * NP + p
                h, c = k // 3, k % 3
                pe.wait_ge(prob_ready, g * CPP + (7 if h == 0 else 8))
                if not (first(b, p, 1) and k < 2):
                    pe.wait_ge(pt_evac[k % 2], g * 3 + k // 2)
                for key, at in PT_CHUNKS[c]:
                    for qi in range(key, TB):
                        ins = pe.transpose(PT[k % 2][:, at + (qi - key) * P:at + (qi - key + 1) * P],
                                           prob[:, p % 2, h, Q_AT[qi] + key * P:Q_AT[qi] + (key + 1) * P], ident[:])
                ins.then_inc(pt_full[k % 2], 1)

            def times_v(b, p):
                g = b * NP + p
                for e in range(2):
                    pe.wait_ge(pt_evac[e], g * 3 + 3)
                if not first(b, p, 1):
                    pe.wait_ge(z_ready, g)
                for key in range(TB):
                    w = S - key * P
                    for h in range(2):
                        cols = slice(p * P + h * DH, p * P + (h + 1) * DH)
                        ins = pe.matmul(ZT[h * DH:(h + 1) * DH, key * P:S], v_sb[:, key, cols],
                                        probT[:, p % 2, h, PT_OF_KEY[key]:PT_OF_KEY[key] + w],
                                        start=(key == 0), stop=(key == TB - 1))
                ins.then_inc(pv_done, 1)

            def out_proj(tiles, bank):
                for n, t in enumerate(tiles):
                    for p in range(NP):
                        ins = pe.matmul(bank[:, n * P:(n + 1) * P], zT[:, p, t * P:(t + 1) * P], wo[:, p, :],
                                        start=(p == 0), stop=(p == NP - 1))
                return ins

            def step(b, p):
                nb, nxt = (b, p + 1) if p + 1 < NP else (b + 1, 0)
                for k in range(2):
                    use = k if first(b, p, 1) else misc(*before(b, p, 1), "kq"[k])
                    pe.wait_ge(misc_free, use + 1)
                before_1 = not first(b, p, 1)
                scores(b, p, 3)
                if p == 2 and not first(b, p, NP):
                    pe.wait_ge(misc_free, misc(b, p, "out"))
                    out_proj((2, 3), MISC).then_inc(misc_full, 1)
                scores(b, p, 2)
                if first(b, p, 1):
                    pe.wait_ge(resid_done, B)
                if not last(b, p):
                    project_qk(nb, nxt, 1, misc(b, p, "k"))
                if first(b, p, 2):
                    pe.wait_ge(xcur_in, 32)
                    if p == 1:
                        pe.wait_ge(v_first_read, 1)
                    project_v(p, 0, ZT).then_inc(v_first_full, 1)
                else:
                    if first(b, p, 3):
                        pe.wait_ge(v_first_read, 2)
                    times_v(*before(b, p, 2))
                if not last(b, p):
                    project_qk(nb, nxt, 0, misc(b, p, "q"))
                if before_1:
                    transposes(*before(b, p, 1), 0)
                    transposes(*before(b, p, 1), 1)
                scores(b, p, 1)
                if before_1:
                    transposes(*before(b, p, 1), 2)
                scores(b, p, 0)
                if before_1:
                    transposes(*before(b, p, 1), 3)
                if not (last_b(b) and p >= 6):
                    if p == 6:
                        pe.wait_ge(xcur_in, b * 32 + 64)
                    half, t = (1, p - 2) if 2 <= p <= 5 else (0, (p - 6) % NP)
                    pe.wait_ge(misc_free, misc(b, p, "v"))
                    project_v(t, half).then_inc(misc_full, 1)
                if before_1:
                    transposes(*before(b, p, 1), 4)
                    transposes(*before(b, p, 1), 5)
                if p == 1 and not first(b, p, NP):
                    pe.wait_ge(misc_free, misc(b, p, "out"))
                    pe.wait_ge(z_ready, b * NP)
                    out_proj((0, 1), MISC).then_inc(misc_full, 1)
                if first(b, p, PEELED) and p in (3, 5):
                    pe.wait_ge(normed, TB * norms_up_to(1, p - 2, 1))
                    pe.wait_ge(misc_free, misc(0, p, "x"))
                    transpose_tiles(MISC, lambda t: x_norm2[:, (p - 2) * TB + t, :]).then_inc(misc_full, 1)

            pe.wait_ge(ident_ready, 1)
            pe.wait_ge(rows_in, 16 * 10)
            pe.transpose(banks[7][:, 0:NCONST], const_rows[:], ident[0:NCONST, 0:NCONST]).then_inc(consts_T, 1)
            pe.wait_ge(consts_ready, 1)
            front_transposes(0, 0)
            pe.wait_ge(wdense_in, 32)
            attn_dense(0, 0)
            ffn_from_experts(0)
            pe.wait_ge(wsplit_ready, 3)
            pe.wait_ge(xhi_ready, 1)
            pe.wait_ge(xlo_ready, 1)
            project_qk(0, 0, 1, None, banks[4])
            next_dense(0, 1)
            project_qk(0, 0, 0, None, banks[5])
            back(0, 1)
            pe.wait_ge(normed, TB * norms_up_to(1, 2, 1))
            transpose_tiles(banks[6], lambda t: x_norm2[:, 2 * TB + t, :]).then_inc(xin_full, 1)
            pe.wait_ge(wo_in, 16)
            walk(pe, step)
            pe.wait_ge(s_masked, G * CPP)
            front_transpose(1, 0, 0, 0)
            front_transpose(1, 0, 1, 0)
            times_v(B - 1, NP - 2)
            transposes(B - 1, NP - 1, 0)
            transposes(B - 1, NP - 1, 1)
            front_transpose(1, 0, 0, 1)
            front_transpose(1, 0, 1, 1)
            for k in range(2, 6):
                transposes(B - 1, NP - 1, k)
            attn_dense(1, 0)
            times_v(B - 1, NP - 1)
            ffn_from_experts(1)
            next_dense(1, 1)
            back(1, 1)


_INS = ['L0_attn_resid_stream', 'L0_attn_W_q', 'L0_attn_W_k', 'L0_attn_W_v', 'L0_attn_W_o', 'L0_attn_b_q',
        'L0_attn_b_k', 'L0_attn_b_v', 'L0_attn_b_o', 'L0_attn_ln_w', 'L0_attn_ln_b', 'L0_ffn_ln_g', 'L0_ffn_ln_b',
        'L0_ffn_attn_w', 'L0_ffn_attn_b', 'L0_ffn_w1', 'L0_ffn_b1', 'L0_ffn_w2', 'L0_ffn_b2', 'L0_ffn_next_w',
        'L0_ffn_next_b']


def kernel(**inputs):
    import numpy as _np
    import concourse.bacc as _bacc
    from concourse import mybir as _mybir
    from concourse.bass_utils import run_bass_kernel_spmd as _run

    nc = _bacc.Bacc("TRN2", target_bir_lowering=False, num_devices=1)
    arrays, args = {}, []
    for name in _INS:
        a = _np.ascontiguousarray(inputs[name])
        arrays[f"in_{name}"] = a
        args.append(nc.dram_tensor(f"in_{name}", a.shape, _mybir.dt.from_np(a.dtype), kind="ExternalInput").ap())
    shape = inputs['L0_attn_resid_stream'].shape
    args.append(nc.dram_tensor("out_x", shape, _mybir.dt.float32, kind="ExternalOutput").ap())
    macaron_kernel(nc, *args)
    r = _run(nc, [arrays], core_ids=[0])
    return r.results[0]["out_x"]
```
